# Optimizing a Trainium2 kernel written in Bass

```python
import numpy as np
import jax
import jax.numpy as jnp

def _softmax(x, axis=-1):
    return jax.nn.softmax(x, axis=axis)

def _gelu(x):
    return jax.nn.gelu(x, approximate=True)

def _silu(x):
    return jax.nn.silu(x)

def _sigmoid(x):
    return jax.nn.sigmoid(x)

def _layernorm(x, axis=-1, eps=1e-05):
    m = jnp.mean(x, axis=axis, keepdims=True)
    v = jnp.var(x, axis=axis, keepdims=True)
    return (x - m) / jnp.sqrt(v + eps)

def _scatter_add(tgt, idx, src, axis=0):
    return tgt.at[idx].add(src)

def _segment_sum(src, seg, n):
    return jax.ops.segment_sum(src, seg, n)
kernel_name = 'mk_prb_d2_jaxref_r8_a9221c'

def setup_inputs(seed: int=0):
    np.random.seed(seed)
    _w = jnp.asarray

    def _L0_attn_setup():
        import jax, jax.numpy as jnp
        import numpy as np
        B, S, D, H = (2, 256, 256, 16)
        HD = D // H
        SCALE = 1.0 / np.sqrt(D).astype(np.float32)
        key = jax.random.key(seed)
        k1, k2, k3 = jax.random.split(key, 3)
        x = jax.random.normal(k1, (B, S, D), dtype=jnp.float32)
        W_qkv = jax.random.normal(k2, (3 * D, D), dtype=jnp.float32) * (1.0 / np.sqrt(D))
        W_proj = jax.random.normal(k3, (D, D), dtype=jnp.float32) * (1.0 / np.sqrt(D))
        return {'x': x, 'W_qkv': W_qkv, 'W_proj': W_proj}
    _L0_attn_in = _L0_attn_setup()

    def _L0_ffn_setup():
        import jax, jax.numpy as jnp
        import numpy as np
        HIDDEN = 256
        INTER = 688
        LUT_SIZE = 16

        def _ghost_linear(x, idx, lut):
            w = lut[idx]
            return jnp.einsum('bsh,oh->bso', x, w)
        key = jax.random.key(seed)
        k_x, k_lut, k_g, k_u, k_d = jax.random.split(key, 5)
        x = jax.random.normal(k_x, (2, 512, HIDDEN), dtype=jnp.float32)
        lut = jax.random.normal(k_lut, (LUT_SIZE,), dtype=jnp.float32) * 0.02
        gate_idx = jax.random.randint(k_g, (INTER, HIDDEN), 0, LUT_SIZE, dtype=jnp.int32)
        up_idx = jax.random.randint(k_u, (INTER, HIDDEN), 0, LUT_SIZE, dtype=jnp.int32)
        down_idx = jax.random.randint(k_d, (HIDDEN, INTER), 0, LUT_SIZE, dtype=jnp.int32)
        return {'x': x, 'lut': lut, 'gate_idx': gate_idx, 'up_idx': up_idx, 'down_idx': down_idx}
    _L0_ffn_in = _L0_ffn_setup()

    def _L1_attn_setup():
        import jax, jax.numpy as jnp
        import numpy as np
        import math
        H = 256
        NH = 16
        HD = H // NH
        THETA = 10000.0

        def rotate_half(x):
            x1, x2 = (x[..., :HD // 2], x[..., HD // 2:])
            return jnp.concatenate((-x2, x1), axis=-1)

        def rope_tables(seq_len, dtype):
            inv_freq = 1.0 / THETA ** (np.arange(0, HD, 2, dtype=np.float32) / HD)
            t = np.arange(seq_len, dtype=np.float32)
            freqs = np.einsum('i,j->ij', t, inv_freq)
            emb = np.concatenate((freqs, freqs), axis=-1)
            return (jnp.asarray(np.cos(emb), dtype), jnp.asarray(np.sin(emb), dtype))
        key = jax.random.key(seed)
        ks = jax.random.split(key, 5)
        B, S = (2, 256)
        scale = 1.0 / math.sqrt(H)
        return {'hidden_states': jax.random.normal(ks[0], (B, S, H), jnp.float32), 'Wq': jax.random.normal(ks[1], (H, H), jnp.float32) * scale, 'Wk': jax.random.normal(ks[2], (H, H), jnp.float32) * scale, 'Wv': jax.random.normal(ks[3], (H, H), jnp.float32) * scale, 'Wo': jax.random.normal(ks[4], (H, H), jnp.float32) * scale}
    _L1_attn_in = _L1_attn_setup()

    def _L1_ffn_setup():
        import jax, jax.numpy as jnp
        import numpy as np
        E = 8
        K = 2
        C = 256
        I = 176
        IS = I * 2
        B, T = (2, 256)
        key = jax.random.key(seed)
        ks = jax.random.split(key, 9)
        s = 0.02
        return {'x': jax.random.normal(ks[0], (B, T, C), dtype=jnp.float32), 'gate_w': jax.random.normal(ks[1], (E, C), dtype=jnp.float32) * s, 'w1': jax.random.normal(ks[2], (E, I, C), dtype=jnp.float32) * s, 'w2': jax.random.normal(ks[3], (E, I, C), dtype=jnp.float32) * s, 'w3': jax.random.normal(ks[4], (E, C, I), dtype=jnp.float32) * s, 'sw1': jax.random.normal(ks[5], (IS, C), dtype=jnp.float32) * s, 'sw2': jax.random.normal(ks[6], (IS, C), dtype=jnp.float32) * s, 'sw3': jax.random.normal(ks[7], (C, IS), dtype=jnp.float32) * s}
    _L1_ffn_in = _L1_ffn_setup()
    _d = {'L0_attn_x': _L0_attn_in['x'], 'L0_attn_W_qkv': _L0_attn_in['W_qkv'], 'L0_attn_W_proj': _L0_attn_in['W_proj'], 'L0_ffn_lut': _L0_ffn_in['lut'], 'L0_ffn_gate_idx': _L0_ffn_in['gate_idx'], 'L0_ffn_up_idx': _L0_ffn_in['up_idx'], 'L0_ffn_down_idx': _L0_ffn_in['down_idx'], 'L1_attn_Wq': _L1_attn_in['Wq'], 'L1_attn_Wk': _L1_attn_in['Wk'], 'L1_attn_Wv': _L1_attn_in['Wv'], 'L1_attn_Wo': _L1_attn_in['Wo'], 'L1_ffn_gate_w': _L1_ffn_in['gate_w'], 'L1_ffn_w1': _L1_ffn_in['w1'], 'L1_ffn_w2': _L1_ffn_in['w2'], 'L1_ffn_w3': _L1_ffn_in['w3'], 'L1_ffn_sw1': _L1_ffn_in['sw1'], 'L1_ffn_sw2': _L1_ffn_in['sw2'], 'L1_ffn_sw3': _L1_ffn_in['sw3']}
    _x0 = _d['L0_attn_x']
    _d['L0_attn_x'] = jax.random.normal(jax.random.fold_in(jax.random.key(seed), 1), (16, 256, 256), dtype=_x0.dtype)
    del _x0
    return _d

def reference(L0_attn_x, L0_attn_W_qkv, L0_attn_W_proj, L0_ffn_lut, L0_ffn_gate_idx, L0_ffn_up_idx, L0_ffn_down_idx, L1_attn_Wq, L1_attn_Wk, L1_attn_Wv, L1_attn_Wo, L1_ffn_gate_w, L1_ffn_w1, L1_ffn_w2, L1_ffn_w3, L1_ffn_sw1, L1_ffn_sw2, L1_ffn_sw3):

    def _L0_attn_ref(x, W_qkv, W_proj):
        import jax, jax.numpy as jnp
        import numpy as np
        B, S, D, H = (2, 256, 256, 16)
        HD = D // H
        SCALE = 1.0 / np.sqrt(D).astype(np.float32)
        b, s, d = x.shape
        qkv = x @ W_qkv.T
        q, k, v = jnp.split(qkv, 3, axis=-1)
        q = q.reshape(b, s, H, HD).transpose(0, 2, 1, 3)
        k = k.reshape(b, s, H, HD).transpose(0, 2, 1, 3)
        v = v.reshape(b, s, H, HD).transpose(0, 2, 1, 3)
        attn = jnp.einsum('bhqd,bhkd->bhqk', q, k) * SCALE
        causal = jnp.tril(jnp.ones((s, s), dtype=bool))
        attn = jnp.where(causal[None, None], attn, -jnp.inf)
        probs = jax.nn.softmax(attn, axis=-1)
        out = jnp.einsum('bhqk,bhkd->bhqd', probs, v)
        out = out.transpose(0, 2, 1, 3).reshape(b, s, d)
        return out @ W_proj.T

    def _L0_ffn_ref(x, lut, gate_idx, up_idx, down_idx):
        import jax, jax.numpy as jnp
        import numpy as np
        HIDDEN = 256
        INTER = 688
        LUT_SIZE = 16

        def _ghost_linear(x, idx, lut):
            w = lut[idx]
            return jnp.einsum('bsh,oh->bso', x, w)
        gate = _ghost_linear(x, gate_idx, lut)
        up = _ghost_linear(x, up_idx, lut)
        h = jax.nn.silu(gate) * up
        return _ghost_linear(h, down_idx, lut)

    def _L1_attn_ref(hidden_states, Wq, Wk, Wv, Wo):
        import jax, jax.numpy as jnp
        import numpy as np
        import math
        H = 256
        NH = 16
        HD = H // NH
        THETA = 10000.0

        def rotate_half(x):
            x1, x2 = (x[..., :HD // 2], x[..., HD // 2:])
            return jnp.concatenate((-x2, x1), axis=-1)

        def rope_tables(seq_len, dtype):
            inv_freq = 1.0 / THETA ** (np.arange(0, HD, 2, dtype=np.float32) / HD)
            t = np.arange(seq_len, dtype=np.float32)
            freqs = np.einsum('i,j->ij', t, inv_freq)
            emb = np.concatenate((freqs, freqs), axis=-1)
            return (jnp.asarray(np.cos(emb), dtype), jnp.asarray(np.sin(emb), dtype))
        B, S, _ = hidden_states.shape

        def proj(W):
            y = jnp.einsum('bsh,oh->bso', hidden_states, W)
            return y.reshape(B, S, NH, HD).transpose(0, 2, 1, 3)
        q, k, v = (proj(Wq), proj(Wk), proj(Wv))
        cos, sin = rope_tables(S, hidden_states.dtype)
        cos, sin = (cos[None, None], sin[None, None])
        q = q * cos + rotate_half(q) * sin
        k = k * cos + rotate_half(k) * sin
        scores = jnp.einsum('bhqd,bhkd->bhqk', q, k) / math.sqrt(HD)
        causal = jnp.triu(jnp.ones((S, S), bool), k=1)
        scores = jnp.where(causal, -jnp.inf, scores)
        attn = jax.nn.softmax(scores, axis=-1)
        out = jnp.einsum('bhqk,bhkd->bhqd', attn, v)
        out = out.transpose(0, 2, 1, 3).reshape(B, S, H)
        return jnp.einsum('bsh,oh->bso', out, Wo)

    def _L1_ffn_ref(x, gate_w, w1, w2, w3, sw1, sw2, sw3):
        import jax, jax.numpy as jnp
        import numpy as np
        E = 8
        K = 2
        C = 256
        I = 176
        IS = I * 2
        B, T = (2, 256)
        Bq, Tq, Cq = x.shape
        xf = x.reshape(-1, Cq)
        logits = xf @ gate_w.T
        probs = jax.nn.softmax(logits.astype(jnp.float32), axis=-1)
        topk_p, topk_i = jax.lax.top_k(probs, K)
        comb = (jax.nn.one_hot(topk_i, E, dtype=jnp.float32) * topk_p[..., None]).sum(axis=1).astype(x.dtype)
        h1 = jnp.einsum('nc,eic->eni', xf, w1)
        h2 = jnp.einsum('nc,eic->eni', xf, w2)
        h = jax.nn.silu(h1) * h2
        eo = jnp.einsum('eni,eci->enc', h, w3)
        y = jnp.einsum('enc,ne->nc', eo, comb).reshape(Bq, Tq, Cq)
        sh = jax.nn.silu(xf @ sw1.T) * (xf @ sw2.T) @ sw3.T
        return y + sh.reshape(Bq, Tq, Cq)
    x = L0_attn_x
    xn = _layernorm(x, axis=-1)
    x = x + _L0_attn_ref(xn, L0_attn_W_qkv, L0_attn_W_proj) + _L0_ffn_ref(xn, L0_ffn_lut, L0_ffn_gate_idx, L0_ffn_up_idx, L0_ffn_down_idx)
    xn = _layernorm(x, axis=-1)
    x = x + _L1_attn_ref(xn, L1_attn_Wq, L1_attn_Wk, L1_attn_Wv, L1_attn_Wo) + _L1_ffn_ref(xn, L1_ffn_gate_w, L1_ffn_w1, L1_ffn_w2, L1_ffn_w3, L1_ffn_sw1, L1_ffn_sw2, L1_ffn_sw3)
    return x

_drawn_inputs = setup_inputs


def setup_inputs(seed=0):
    import zlib

    import numpy as np

    out = dict(_drawn_inputs(seed))
    spreads = {}
    factors = {'L1_ffn_gate_w': 8.0,
     'L1_ffn_w1': 8.0,
     'L1_ffn_w2': 8.0,
     'L1_ffn_w3': 8.0,
     'L1_ffn_sw1': 3.022,
     'L1_ffn_sw2': 2.993,
     'L1_ffn_sw3': 2.992}
    for name, (base, spread) in spreads.items():
        noise = np.random.default_rng([zlib.crc32(name.encode()), seed]).standard_normal(out[name].shape)
        drawn = base * np.exp(spread * noise) if base else spread * noise
        out[name] = jnp.asarray(drawn.astype(out[name].dtype))
    for name, factor in factors.items():
        out[name] = (out[name] * factor).astype(out[name].dtype)
    return out
```

```python
from contextlib import ExitStack

import numpy as np

import concourse.bass as bass
from concourse import mybir

F32 = mybir.dt.float32
F32R = mybir.dt.float32r
BF16 = mybir.dt.bfloat16
I32 = mybir.dt.int32
U32 = mybir.dt.uint32
ALU = mybir.AluOpType
ACT = mybir.ActivationFunctionType
AX = mybir.AxisListType

P = 128
B = 16
S = 256
D = 256
KT = D // P
BLK = S // P
H = 16
HD = D // H
NPAIR = H // 2
LUT = 16
INTER = 688
NE = 8
EI = 176
SI = 352
T0 = -(-INTER // P)
TS = -(-SI // P)
TE = NE * EI // P
NF = (T0, TS + TE)
SCALE = (1.0 / 16.0, 1.0 / 4.0)
EPS = 1e-5

GU_TILE = KT * 2 * P
N_GU0, N_DN0 = T0 * GU_TILE, T0 * D
N_GU1, N_DN1 = NF[1] * GU_TILE, NF[1] * D
N_QKV, N_WO, N_ROT, N_RT = KT * 3 * D, KT * D, KT * 2 * D, KT * P
N_STREAM = N_QKV + N_RT + N_GU1
STREAM_CHUNK = N_STREAM // B
LATE_CHUNK = 512
SLOT = STREAM_CHUNK
N_SLOTS = 5

LUT_PIECE = 1024
LUT_PIECES = [("A", 0, 1024), ("A", 1024, 1024), ("A", 2048, 1024), ("C", 0, 1024), ("C", 1024, 512)]
LATE = [("B", c, N_DN1 + c) for c in range(0, N_QKV, LATE_CHUNK)] \
    + [("A", c, c) for c in range(0, N_GU0, LATE_CHUNK)] + [("A", N_GU0, N_GU0)]
N_LATE_B = N_QKV // LATE_CHUNK
LATE_SLOTS = 3
N_CONST, N_CONST_SET = 6, 6


def late_for_dn(f):
    return N_LATE_B + (f * D) // LATE_CHUNK + 1


STEPS = (
    ["QK", "V", ("F", 0), ("F", 1), "LNS", ("F", 2)]
    + [("MAX", j) for j in range(4)] + [("F", 3)] + [("MAX", j) for j in range(4, 8)]
    + ["NM", "LNN", ("F", 4), ("F", 5)]
    + [("ST", j) for j in range(9)]
    + ["TR", "X", ("F", 6), "OT", ("F", 7), "PROJ"],
    ["QK", "ROT", "VR", ("F", 0), "LT", ("F", 1), ("F", 2), "CT", ("F", 3), "CB0", "CB1", "CB2", "LNS"]
    + [("MAX", 0), ("MAX", 1), ("F", 4), ("MAX", 2), ("MAX", 3), ("F", 5), ("MAX", 4), ("MAX", 5), ("F", 6),
       ("MAX", 6), ("MAX", 7), ("F", 7), "NM", "LNN", ("F", 8), ("F", 9)]
    + [("ST", 0), ("ST", 1), ("F", 10), ("ST", 2), ("ST", 3), ("F", 11), ("ST", 4), ("ST", 5), ("F", 12),
       ("ST", 6), ("ST", 7), ("ST", 8), ("F", 13)]
    + ["TR", "X", ("F", 14), "OT", ("F", 15), "PROJ"],
)
UNITS = (
    ["X", "QK", "V"] + [("MAX", j) for j in range(8)] + ["NM"] + [("ST", j) for j in range(8)] + ["TR", "OT"],
    ["X", "QK", "ROT", "VR", "LT", "CT", "CB0", "CB1", "CB2"] + [("MAX", j) for j in range(8)] + ["NM"]
    + [("ST", j) for j in range(8)] + ["TR", "OT"],
)
assert all(len(u) % 2 == 0 for u in UNITS)

CREDIT = 3


class Counter:

    def __init__(self, handle, per, by=1):
        self.handle, self.per, self.by = handle, per, by

    def at(self, layer, b, k):
        if layer == 0:
            return b * (self.per[0] * self.by) + (CREDIT + k) * self.by
        return b * (self.per[1] * self.by) + (CREDIT + B * self.per[0] + k) * self.by


def build(nc, x_in, w0_lin, idx0, lut_in, w1_stream, w1_late, rope_in, ident_in, mask_in, esel_in, iota_in, y_out):
    x1 = nc.dram_tensor("x1_scratch", (B, BLK, P, D), F32, kind="Internal").ap()
    src = (x_in.rearrange("b (k p) d -> b p k d", p=P), x1.rearrange("b k p d -> b p k d"))
    dst = (x1.rearrange("b k p d -> b p k d"), y_out.rearrange("b (k p) d -> b p k d", p=P))

    with ExitStack() as ctx:
        def sb(name, shape, dt=F32):
            return ctx.enter_context(nc.sbuf_tensor(name, shape, dt))

        counters = []

        def counter(name, per, by=1):
            c = Counter(ctx.enter_context(nc.semaphore(name)), per, by)
            counters.append(c)
            return c

        def sem(name):
            return ctx.enter_context(nc.semaphore(name))

        wA = sb("wA", [P, 2, N_DN1], F32R)
        wB = sb("wB", [P, 2, N_QKV], F32R)
        wC = sb("wC", [P, 2, N_DN0], F32R)
        wD = sb("wD", [P, 2, N_STREAM], F32R)
        assert N_GU0 + N_WO == N_DN1 and N_ROT + N_WO == N_QKV
        GU = (wA[:, :, 0:N_GU0].rearrange("p s (f k g c) -> p s f k g c", f=T0, k=KT, g=2),
              wD[:, :, N_QKV + N_RT:].rearrange("p s (f k g c) -> p s f k g c", f=NF[1], k=KT, g=2))
        DN = (wC[:, :, :].rearrange("p s (f c) -> p s f c", f=T0), wA[:, :, :].rearrange("p s (f c) -> p s f c", f=NF[1]))
        QKV = (wB[:, :, :].rearrange("p s (k c) -> p s k c", k=KT), wD[:, :, 0:N_QKV].rearrange("p s (k c) -> p s k c", k=KT))
        WO = (wA[:, :, N_GU0:].rearrange("p s (k c) -> p s k c", k=KT), wB[:, :, N_ROT:].rearrange("p s (k c) -> p s k c", k=KT))
        ROTW = wB[:, :, 0:N_ROT].rearrange("p s (k c) -> p s k c", k=KT)
        RTW = wD[:, :, N_QKV:N_QKV + N_RT].rearrange("p s (k c) -> p s k c", k=KT)

        ident = sb("ident", [P, P])
        identb = sb("identb", [P, P], BF16)
        maskb = sb("maskb", [P, 2, P], BF16)
        rope = sb("rope", [P, 2, S])
        esel = sb("esel", [64, TE, P], F32R)
        iota = sb("iota", [P, NE])
        lut = sb("lut", [P, LUT])
        negh = sb("negh", [P, BLK])

        xt = sb("xt", [P, 2, BLK, D])
        stats = sb("stats", [P, BLK, 6])
        mv = sb("mv", [P, BLK, 2])
        vareps = sb("vareps", [P, BLK])
        rstd = sb("rstd", [P, BLK])
        xn = sb("xn", [P, BLK, D])
        xT = sb("xT", [P, 2, KT, S], F32R)
        split = sb("split", [P, 4, 2, S])
        stk = sb("stk", [P, 2, NPAIR, S], F32R)
        stkf = stk[:, :, :, :].bitcast(F32)
        vaug = sb("vaug", [P, BLK, H, 2 * HD])
        mx = sb("mx", [P, BLK, H])
        nmT = sb("nmT", [H, S])
        nmTr = nmT[:, :].bitcast(F32R)
        prob = sb("prob", [P, 2, 3, 2, P])
        pvT = sb("pvT", [P, 4, S])
        rden = sb("rden", [P, BLK, H])
        o_tok = pvT[:, 0:2, :]
        oT = sb("oT", [P, 2, KT, S], F32R)
        th = sb("th", [P, 2, S])
        ga = sb("ga", [P, 2, S])
        hb = sb("hb", [P, 2, S])
        hs = sb("hs", [P, 2, 2, S], F32R)
        big = sb("big", [P, N_SLOTS * SLOT + 16])
        combB = big[:, 0:TE * S].rearrange("p (t s) -> p t s", t=TE)
        ropet = prob[:, :, :, :, :].rearrange("p a b c d -> p (a b c d)")[:, 0:4 * S].rearrange("p (a s) -> p a s", a=4)
        lgT = nmT[0:NE, :]
        lg = sb("lg", [P, BLK, NE])
        m8 = sb("m8", [P, BLK, 8])
        i8 = sb("i8", [P, BLK, 8], U32)
        i8f = sb("i8f", [P, BLK, 8])
        nmax = sb("nmax", [P, BLK])
        ex = sb("ex", [P, BLK, NE])
        esum = sb("esum", [P, BLK])
        rsum = sb("rsum", [P, BLK])
        sel0 = sb("sel0", [P, BLK, NE])
        sel1 = sb("sel1", [P, BLK, NE])
        comb = sb("comb", [P, BLK, 40])
        combT = sb("combT", [40, S], F32R)

        pair = [ctx.enter_context(nc.psum_tensor(f"pair{n}", [P, 2, 512], F32)) for n in "ab"]
        pv = ctx.enter_context(nc.psum_tensor("pv", [P, 2, S], F32))
        acc = ctx.enter_context(nc.psum_tensor("acc", [P, BLK, D], F32))
        gu = [ctx.enter_context(nc.psum_tensor(f"gu{n}", [P, 2, S], F32)) for n in range(2)]

        unit_ready = counter("unit_ready", (len(UNITS[0]), len(UNITS[1])))
        pair_done = [counter(f"pair_done_{n}", (len(UNITS[0]) // 2, len(UNITS[1]) // 2)) for n in "ab"]
        ln_stats = counter("ln_stats", (4, 4))
        ln_rstd = counter("ln_rstd", (2, 2))
        xn_done = counter("xn_done", (1, 1))
        x_hi = counter("x_hi", (1, 1))
        qk_hi = counter("qk_hi", (1, 1))
        qk_lo = counter("qk_lo", (0, 1))
        rope_sum = counter("rope_sum", (0, 1))
        stk_loaded = counter("stk_loaded", (24, 24), 16)
        nm_loaded = counter("nm_loaded", (2, 2), 16)
        masked = counter("masked", (8, 8))
        pv_done = counter("pv_done", (8, 8))
        pv_out = counter("pv_out", (4, 4))
        den_done = counter("den_done", (1, 1))
        o_hi = counter("o_hi", (1, 1))
        gu_ready = counter("gu_ready", NF)
        tanh_done = counter("tanh_done", NF)
        gate_done = counter("gate_done", NF)
        hid_done = counter("hid_done", NF)
        weighted = counter("weighted", (0, TE))
        h_hi = counter("h_hi", NF)
        h_lo = counter("h_lo", NF)
        dn_done = counter("dn_done", NF)
        acc_ready = counter("acc_ready", (1, 1))
        y_done = counter("y_done", (1, 1))
        top_step = counter("top_step", (0, 11))
        exps_done = counter("exps_done", (0, 2))
        comb_done = counter("comb_done", (0, 4))
        comb_hi = counter("comb_hi", (0, 1))
        MADE_BY = {
            "PE": (unit_ready, pv_done, gu_ready, dn_done, acc_ready),
            "ACT": (x_hi, qk_hi, o_hi, tanh_done, h_hi, exps_done, comb_hi),
            "DVE": (pair_done[0], pair_done[1], ln_stats, xn_done, qk_lo, pv_out, den_done, gate_done, hid_done,
                    h_lo, y_done, top_step, comb_done),
            "POOL": (ln_rstd, rope_sum, masked, weighted),
            "SP": (stk_loaded, nm_loaded),
        }
        assert sorted(id(c) for v in MADE_BY.values() for c in v) == sorted(id(c) for c in counters)
        x_loaded = [sem(f"x_loaded{n}") for n in range(2)]
        y_stored = [sem(f"y_stored{n}") for n in range(2)]
        raw_loaded = [sem(f"raw_loaded{n}") for n in range(2)]
        raw_hi, raw_lo = sem("raw_hi"), sem("raw_lo")
        late_loaded = [sem(f"late_loaded{n}") for n in range(LATE_SLOTS)]
        late_hi, late_lo = sem("late_hi"), sem("late_lo")
        const_loaded, const_hi, const_set = sem("const_loaded"), sem("const_hi"), sem("const_set")
        w0_loaded, w0_hi, w0_lo = sem("w0_loaded"), sem("w0_hi"), sem("w0_lo")
        idx_loaded = [sem(f"idx_loaded{n}") for n in range(2)]
        lut_step = sem("lut_step")
        dve_passed, pool_passed, sp_passed = sem("dve_passed"), sem("pool_passed"), sem("sp_passed")

        def prime(eng, who):
            for c in MADE_BY[who]:
                eng.sem_inc(c.handle, CREDIT * c.by)

        def wait(eng, c, layer, b, k):
            eng.wait_ge(c.handle, c.at(layer, b, k))

        def alone(eng, passed):
            eng.sem_inc(passed, 1)

        def unit(layer, what):
            j = UNITS[layer].index(what)
            return j, j % 2, j // 2

        def unit_filled(eng, layer, b, what):
            wait(eng, unit_ready, layer, b, unit(layer, what)[0] + 1)

        def unit_read(eng, layer, b, what):
            _, p, turn = unit(layer, what)
            wait(eng, pair_done[p], layer, b, turn + 1)

        def banks_free(eng, layer, b, what):
            _, p, turn = unit(layer, what)
            wait(eng, pair_done[p], layer, b, turn)

        def banks(layer, what):
            return pair[unit(layer, what)[1]]

        def read_out(layer, what):
            return pair_done[unit(layer, what)[1]].handle

        def stored_before(layer, b, n):
            return (b - n) * (16 // 2) + 16 * (1 + layer * (B // 2) + n)

        def loaded_by(layer, b, n):
            return (b - n) * (16 // 2) + 16 * (1 + layer * (B // 2))

        def walk(eng, step):
            for layer in range(2):
                with eng.Fori(0, B // 2 - 1) as i:
                    for n in range(2):
                        b = i * 2 + n
                        step(layer, b, n, (layer, b + 1, 1 - n))
                step(layer, B - 2, 0, (layer, B - 1, 1))
                step(layer, B - 1, 1, (1, 0, 0) if layer == 0 else None)

        def last_of_layer0(layer, b):
            return layer == 0 and isinstance(b, int) and b == B - 1

        def dram_batch(view, b):
            return view[bass.ds(b, 1)].rearrange("a p k d -> (a p) k d")

        def flat(t, n, dt=None):
            dims = " ".join("abcde"[:len(t.shape) - 1])
            v = t[tuple(slice(None) for _ in t.shape)]
            v = v.rearrange(f"p {dims} -> p ({dims})") if len(t.shape) > 2 else v
            v = v[:, 0:n]
            return v.bitcast(dt) if dt is not None else v

        def store(w):
            return {"A": wA, "B": wB, "C": wC}[w]

        def late_slot(c):
            s = 2 + c % LATE_SLOTS
            return big[:, s * SLOT:s * SLOT + LATE_CHUNK]

        def idx_slot(c, n):
            return flat(split, 2048, I32)[:, (c % 2) * LUT_PIECE:(c % 2) * LUT_PIECE + n]

        block = ctx.enter_context(nc.Block())

        @block.sync
        def _(sp):
            prime(sp, "SP")
            for n in range(2):
                sp.sem_inc(y_stored[n], 16)
            sp.dma_start(xt[:, 0, :, :], dram_batch(src[0], 0)).then_inc(x_loaded[0], 16)
            sp.dma_start(lut[:, :], lut_in.partition_broadcast(P)).then_inc(const_loaded, 16)
            sp.dma_start(ident[:, :], ident_in).then_inc(const_loaded, 16)
            sp.dma_start(th[:, 0, :], mask_in).then_inc(const_loaded, 16)
            sp.dma_start(rope[:, :, :], rope_in).then_inc(const_loaded, 16)
            sp.dma_start(iota[:, :], iota_in).then_inc(const_loaded, 16)
            sp.dma_start(flat(prob, TE * P)[0:64], esel_in).then_inc(const_loaded, 16)
            for c, (_, _, n) in enumerate(LUT_PIECES):
                if c >= 2:
                    sp.wait_ge(lut_step, 2 * LUT * (c - 1))
                sp.dma_start(idx_slot(c, n), idx0[:, c * LUT_PIECE:c * LUT_PIECE + n]).then_inc(idx_loaded[c % 2], 16)
                if c == 1:
                    sp.dma_start(big[:, 0:N_QKV], w0_lin[:, 0:N_QKV]).then_inc(w0_loaded, 16)
                    sp.dma_start(big[:, N_QKV:N_QKV + N_WO], w0_lin[:, N_QKV:]).then_inc(w0_loaded, 16)
            sp.wait_ge(w0_lo, 2)

            def step(layer, b, n, nxt):
                for s in STEPS[layer]:
                    if s == "QK":
                        if nxt is not None:
                            nl, nb, m = nxt
                            sp.wait_ge(y_stored[m], stored_before(layer, b, n))
                            alone(sp, sp_passed)
                            sp.dma_start(xt[:, m, :, :], dram_batch(src[nl], nb)).then_inc(x_loaded[m], 16)
                        if layer == 0:
                            unit_read(sp, layer, b, "QK")
                    if s == ("QK" if layer == 0 else "ROT"):
                        if layer == 1:
                            wait(sp, qk_lo, layer, b, 1)
                        alone(sp, sp_passed)
                        wait(sp, pv_done, layer, b, 0)
                        for r in range(2):
                            for jj in range(4):
                                p0 = 32 * jj + 16 * r
                                for c, parts in enumerate((slice(1, 3), slice(0, 3, 2), slice(1, 4, 2))):
                                    q0 = 64 * r + 16 * c
                                    sp.dma_start(stkf[q0:q0 + 16, :, 2 * jj:2 * jj + 2, :],
                                                 split[p0:p0 + 16, parts, :, :]).then_inc(stk_loaded.handle, 16)
                    elif s == "V":
                        sp.wait_ge(raw_lo, b + 1)
                        alone(sp, sp_passed)
                        sp.dma_start(big[:, n * SLOT:n * SLOT + STREAM_CHUNK],
                                     w1_stream[:, bass.ds(b * STREAM_CHUNK, STREAM_CHUNK)])\
                            .then_inc(raw_loaded[n], 16)
                        if last_of_layer0(layer, b):
                            for c in range(LATE_SLOTS):
                                sp.dma_start(late_slot(c), w1_late[:, LATE[c][2]:LATE[c][2] + LATE_CHUNK])\
                                    .then_inc(late_loaded[c % LATE_SLOTS], 16)
                    elif s == "NM":
                        unit_read(sp, layer, b, "NM")
                        for r in range(2):
                            sp.dma_start(stkf[64 * r + 48:64 * r + 49, 0, :, :], nmT[8 * r:8 * r + 8, :])\
                                .then_inc(nm_loaded.handle, 16)
                        if last_of_layer0(layer, b):
                            for c in range(LATE_SLOTS, len(LATE)):
                                sp.wait_ge(late_lo, c - LATE_SLOTS + 1)
                                sp.dma_start(late_slot(c), w1_late[:, LATE[c][2]:LATE[c][2] + LATE_CHUNK])\
                                    .then_inc(late_loaded[c % LATE_SLOTS], 16)
                    elif s == "PROJ":
                        wait(sp, y_done, layer, b, 1)
                        alone(sp, sp_passed)
                        sp.dma_start(dram_batch(dst[layer], b), xt[:, n, :, :]).then_inc(y_stored[n], 16)

            walk(sp, step)
            for n in range(2):
                sp.wait_ge(y_stored[n], 16 * (1 + B))

        @block.tensor
        def _(pe):
            prime(pe, "PE")

            def three(out, lhs, rhs, start, stop=False, **more):
                pe.matmul(out, lhs(0), rhs(0), start=start, stop=False, **more)
                pe.matmul(out, lhs(0), rhs(1), start=False, stop=False, **more)
                return pe.matmul(out, lhs(1), rhs(0), start=False, stop=stop, **more)

            def x_unit(nl, nb):
                wait(pe, xn_done, nl, nb, 1)
                banks_free(pe, nl, nb, "X")
                for kt in range(KT):
                    for blk in range(BLK):
                        mm = pe.transpose(banks(nl, "X")[:, 0, kt * S + blk * P:kt * S + (blk + 1) * P],
                                          xn[:, blk, kt * P:(kt + 1) * P], ident[:, :])
                mm.then_inc(unit_ready.handle, 1)

            pe.wait_ge(const_loaded, 16 * N_CONST)
            x_unit(0, 0)
            pe.wait_ge(const_set, N_CONST_SET)
            pe.wait_ge(const_hi, 1)
            pe.wait_ge(w0_lo, 2 + len(LUT_PIECES))

            def step(layer, b, n, nxt):
                for s in STEPS[layer]:
                    kind, j = s if isinstance(s, tuple) else (s, None)
                    if kind in ("QK", "ROT"):
                        banks_free(pe, layer, b, s)
                        if kind == "QK":
                            unit_read(pe, layer, b, "X")
                            if layer == 1:
                                pe.wait_ge(raw_lo, 2 + B)
                        else:
                            pe.wait_ge(late_lo, N_LATE_B)
                        w = QKV[layer] if kind == "QK" else ROTW
                        for qk in range(2):
                            for t in range(2):
                                for kt in range(KT):
                                    mm = three(banks(layer, s)[:, qk, t * S:(t + 1) * S],
                                               lambda h: w[:, h, kt, (2 * qk + t) * P:(2 * qk + t + 1) * P],
                                               lambda h: xT[:, h, kt, :], start=kt == 0, stop=kt == KT - 1)
                        mm.then_inc(unit_ready.handle, 1)
                    elif kind in ("V", "VR"):
                        banks_free(pe, layer, b, s)
                        for blk in range(BLK):
                            for kt in range(KT):
                                mm = three(banks(layer, s)[:, 0, blk * D:(blk + 1) * D],
                                           lambda h: xT[:, h, kt, blk * P:(blk + 1) * P],
                                           lambda h: QKV[layer][:, h, kt, 2 * D:3 * D], start=kt == 0, stop=kt == KT - 1)
                        if kind == "VR":
                            for kt in range(KT):
                                mm = three(banks(layer, s)[:, 1, 0:S], lambda h: RTW[:, h, kt, :],
                                           lambda h: xT[:, h, kt, :], start=kt == 0, stop=kt == KT - 1)
                        mm.then_inc(unit_ready.handle, 1)
                    elif kind == "LT":
                        banks_free(pe, layer, b, s)
                        unit_read(pe, layer, b, "VR")
                        for blk in range(BLK):
                            mm = pe.matmul(banks(layer, s)[:, 0, blk * NE:(blk + 1) * NE], nmT[0:NE, blk * P:(blk + 1) * P],
                                           ident[0:NE, 0:NE], start=True, stop=True)
                        mm.then_inc(unit_ready.handle, 1)
                    elif kind == "CT":
                        banks_free(pe, layer, b, s)
                        wait(pe, comb_done, layer, b, 4)
                        for blk in range(BLK):
                            mm = pe.matmul(banks(layer, s)[0:40, 0, blk * P:(blk + 1) * P], comb[:, blk, :], ident[:, :],
                                           start=True, stop=True)
                        mm.then_inc(unit_ready.handle, 1)
                    elif kind in ("CB0", "CB1", "CB2"):
                        banks_free(pe, layer, b, s)
                        unit_read(pe, layer, b, "CT")
                        c = int(kind[2])
                        for x, t in enumerate(range(4 * c, min(4 * c + 4, TE))):
                            mm = pe.matmul(banks(layer, s)[:, x // 2, (x % 2) * S:(x % 2 + 1) * S], esel[0:40, t, :],
                                           combT[:, :], start=True, stop=True)
                        mm.then_inc(unit_ready.handle, 1)
                    elif kind == "MAX":
                        banks_free(pe, layer, b, s)
                        if j == 0:
                            wait(pe, stk_loaded, layer, b, 24)
                        for blk in range(BLK):
                            for r in range(2):
                                rows = slice(64 * r, 64 * r + 48)
                                pe.matmul(banks(layer, s)[:, r, blk * S:(blk + 1) * S],
                                          stk[rows, 0, j, blk * P:(blk + 1) * P], stk[rows, 1, j, :],
                                          start=blk == 0, stop=False, skip_group_check=True)
                        for r in range(2):
                            diag = banks(layer, s)[:, r, :].rearrange("p (a c) -> p a c", c=P)[:, 0:4:3, :]
                            mm = pe.matmul(diag, identb[:, :], maskb[:, :, :], start=False, stop=True,
                                           skip_group_check=True)
                        mm.then_inc(unit_ready.handle, 1)
                    elif kind == "NM":
                        banks_free(pe, layer, b, s)
                        unit_read(pe, layer, b, ("MAX", NPAIR - 1))
                        for blk in range(BLK):
                            mm = pe.matmul(banks(layer, s)[0:H, 0, blk * P:(blk + 1) * P], mx[:, blk, :], ident[:, :],
                                           start=True, stop=True)
                        mm.then_inc(unit_ready.handle, 1)
                    elif kind == "ST":
                        if j < NPAIR:
                            banks_free(pe, layer, b, s)
                            if j == 0:
                                wait(pe, nm_loaded, layer, b, 2)
                            for kb in range(BLK):
                                for r in range(2):
                                    rows = slice(64 * r, 64 * r + 49)
                                    mm = pe.matmul(banks(layer, s)[:, r, kb * S:(kb + 1) * S],
                                                   stk[rows, 1, j, kb * P:(kb + 1) * P], stk[rows, 0, j, :],
                                                   start=True, stop=True)
                            mm.then_inc(unit_ready.handle, 1)
                        if j >= 1:
                            u = j - 1
                            wait(pe, masked, layer, b, u + 1)
                            if u % 2 == 0:
                                wait(pe, pv_out, layer, b, u // 2)
                            for r in range(2):
                                h = 2 * u + r
                                rows = slice(32 * (h % 4), 32 * (h % 4) + 32)
                                pe.matmul(pv[rows, 0, :].rearrange("p (a c) -> p a c", a=2), vaug[:, 0, h, :],
                                          prob[:, u % 2, 0:3:2, r, :],
                                          start=True, stop=False, skip_group_check=True)
                                mm = pe.matmul(pv[rows, 0, P:S], vaug[:, 1, h, :], prob[:, u % 2, 1, r, :],
                                               start=False, stop=True, skip_group_check=True)
                            mm.then_inc(pv_done.handle, 1)
                    elif kind == "TR":
                        banks_free(pe, layer, b, s)
                        wait(pe, pv_out, layer, b, 4)
                        for blk in range(BLK):
                            for g in range(4):
                                mm = pe.transpose(banks(layer, s)[:, blk, g * P:(g + 1) * P],
                                                  pvT[:, g, blk * P:(blk + 1) * P], ident[:, :])
                        mm.then_inc(unit_ready.handle, 1)
                    elif kind == "OT":
                        banks_free(pe, layer, b, s)
                        unit_read(pe, layer, b, "TR")
                        for kt in range(KT):
                            for blk in range(BLK):
                                mm = pe.transpose(banks(layer, s)[:, 0, kt * S + blk * P:kt * S + (blk + 1) * P],
                                                  o_tok[:, blk, kt * P:(kt + 1) * P], ident[:, :])
                        mm.then_inc(unit_ready.handle, 1)
                    elif kind == "X":
                        if nxt is not None:
                            x_unit(nxt[0], nxt[1])
                    elif kind == "PROJ":
                        unit_read(pe, layer, b, "OT")
                        for blk in range(BLK):
                            for kt in range(KT):
                                mm = three(acc[:, blk, :], lambda h: oT[:, h, kt, blk * P:(blk + 1) * P],
                                           lambda h: WO[layer][:, h, kt, :], start=False, skip_group_check=True,
                                           stop=blk == BLK - 1 and kt == KT - 1)
                        mm.then_inc(acc_ready.handle, 1)
                    elif kind == "F":
                        if j < NF[layer]:
                            wait(pe, hid_done, layer, b, j - 1)
                            for g in range(2):
                                for kt in range(KT):
                                    mm = three(gu[j % 2][:, g, :], lambda h: GU[layer][:, h, j, kt, g, :],
                                               lambda h: xT[:, h, kt, :], start=kt == 0, stop=kt == KT - 1)
                            mm.then_inc(gu_ready.handle, 1)
                        if j >= 2:
                            f = j - 2
                            wait(pe, h_lo, layer, b, f + 1)
                            if f == 0:
                                wait(pe, y_done, layer, b, 0)
                            if layer == 1:
                                pe.wait_ge(late_lo, late_for_dn(f))
                            for blk in range(BLK):
                                mm = three(acc[:, blk, :], lambda h: hs[:, f % 2, h, blk * P:(blk + 1) * P],
                                           lambda h: DN[layer][:, h, f, :], start=f == 0 and blk == 0,
                                           skip_group_check=True)
                            mm.then_inc(dn_done.handle, 1)

            walk(pe, step)

        @block.scalar
        def _(act):
            prime(act, "ACT")
            act.wait_ge(const_loaded, 16 * N_CONST)
            act.copy(esel[:, :, :].rearrange("p a b -> p (a b)"), flat(prob, TE * P)[0:64]).then_inc(const_hi, 1)
            act.wait_ge(w0_loaded, 32)
            act.copy(wB[:, 0, :], big[:, 0:N_QKV]).then_inc(w0_hi, 1)
            act.copy(wA[:, 0, N_GU0:], big[:, N_QKV:N_QKV + N_WO]).then_inc(w0_hi, 1)

            def x_unit(nl, nb):
                unit_filled(act, nl, nb, "X")
                act.copy(xT[:, 0, :, :].rearrange("p a b -> p (a b)"), banks(nl, "X")[:, 0, :]).then_inc(x_hi.handle, 1)

            x_unit(0, 0)
            for c, (w, at, n) in enumerate(LUT_PIECES):
                act.wait_ge(lut_step, 2 * LUT * (c + 1))
                act.copy(store(w)[:, 0, at:at + n], flat(pvT, n)).then_inc(w0_hi, 1)

            def late(c0, c1):
                for c in range(c0, c1):
                    w, at, _ = LATE[c]
                    act.wait_ge(late_loaded[c % LATE_SLOTS], 16 * (c // LATE_SLOTS + 1))
                    act.copy(store(w)[:, 0, at:at + LATE_CHUNK], late_slot(c)).then_inc(late_hi, 1)

            def step(layer, b, n, nxt):
                for s in STEPS[layer]:
                    kind, j = s if isinstance(s, tuple) else (s, None)
                    if kind == "QK" and layer == 0:
                        unit_filled(act, layer, b, s)
                        wait(act, stk_loaded, layer, b, 0)
                        act.copy(split[:, 1:3, :, :].rearrange("p a b c -> p a (b c)").bitcast(F32R),
                                 banks(layer, s)[:, :, :]).then_inc(qk_hi.handle, 1)
                    elif kind == "ROT":
                        wait(act, rope_sum, layer, b, 1)
                        act.copy(split[:, 1:3, :, :].rearrange("p a b c -> p (a b c)").bitcast(F32R),
                                 ropet.rearrange("p a s -> p (a s)")).then_inc(qk_hi.handle, 1)
                    elif kind in ("V", "VR"):
                        unit_filled(act, layer, b, s)
                        v = act.copy(vaug[:, :, :, 0:HD],
                                     banks(layer, s)[:, 0, :].rearrange("p (k h d) -> p k h d", k=BLK, h=H))
                        if kind == "V":
                            v.then_inc(read_out(layer, s), 1)
                        else:
                            act.copy(lgT, banks(layer, s)[0:NE, 1, 0:S]).then_inc(read_out(layer, s), 1)
                    elif kind == "LT":
                        wait(act, top_step, layer, b, 5)
                        for blk in range(BLK):
                            act.activation(ex[:, blk, :], lg[:, blk, :], ACT.Exp, bias=nmax[:, blk:blk + 1],
                                           accum_out=esum[:, blk:blk + 1]).then_inc(exps_done.handle, 1)
                    elif kind == "CT":
                        unit_filled(act, layer, b, s)
                        act.copy(combT[:, :], banks(layer, s)[0:40, 0, 0:S]).then_inc(comb_hi.handle, 1)
                    elif kind in ("CB0", "CB1", "CB2"):
                        c = int(kind[2])
                        nt = min(4, TE - 4 * c)
                        unit_filled(act, layer, b, s)
                        if c == 0:
                            wait(act, weighted, layer, b, 0)
                            act.wait_ge(late_lo, len(LATE))
                        act.copy(combB[:, 4 * c:4 * c + nt, :].rearrange("p a b -> p (a b)"),
                                 banks(layer, s)[:, :, :].rearrange("p a b -> p (a b)")[:, 0:nt * S])\
                            .then_inc(read_out(layer, s), 1)
                    elif kind == "NM":
                        unit_filled(act, layer, b, s)
                        act.activation(nmT[:, :].bitcast(F32R), banks(layer, s)[0:H, 0, 0:S], ACT.Copy, scale=-1.0)\
                            .then_inc(read_out(layer, s), 1)
                        if layer == 0:
                            act.wait_ge(raw_loaded[n], (b - n) * 8 + 16)
                            act.copy(wD[:, 0, bass.ds(b * STREAM_CHUNK, STREAM_CHUNK)],
                                     big[:, n * SLOT:n * SLOT + STREAM_CHUNK]).then_inc(raw_hi, 1)
                        if last_of_layer0(layer, b):
                            late(0, N_LATE_B)
                    elif kind == "ST" and j < NPAIR:
                        unit_filled(act, layer, b, s)
                        wait(act, pv_done, layer, b, j - 1)
                        act.activation(prob[:, j % 2, 0:3:2, :, :].rearrange("p a r c -> p r a c"),
                                       banks(layer, s)[:, :, 0:S].rearrange("p r (a c) -> p r a c", c=P), ACT.Exp,
                                       scale=SCALE[layer])
                        act.activation(prob[:, j % 2, 1, :, :], banks(layer, s)[:, :, S + P:2 * S], ACT.Exp,
                                       scale=SCALE[layer]).then_inc(read_out(layer, s), 1)
                    elif kind == "OT":
                        unit_filled(act, layer, b, s)
                        act.copy(oT[:, 0, :, :].rearrange("p a b -> p (a b)"), banks(layer, s)[:, 0, :])\
                            .then_inc(o_hi.handle, 1)
                    elif kind == "X" and nxt is not None:
                        x_unit(nxt[0], nxt[1])
                        if last_of_layer0(layer, b):
                            late(N_LATE_B, len(LATE) - 1)
                    elif kind == "PROJ" and last_of_layer0(layer, b):
                        wait(act, acc_ready, layer, b, 1)
                        late(len(LATE) - 1, len(LATE))
                    elif kind == "F":
                        if j < NF[layer]:
                            wait(act, gu_ready, layer, b, j + 1)
                            wait(act, gate_done, layer, b, j - 1)
                            act.activation(th[:, j % 2, :], gu[j % 2][:, 0, :], ACT.Tanh, scale=0.5)\
                                .then_inc(tanh_done.handle, 1)
                        if 1 <= j <= NF[layer]:
                            f = j - 1
                            if layer == 1 and f >= TS:
                                wait(act, weighted, layer, b, f - TS + 1)
                            else:
                                wait(act, hid_done, layer, b, f + 1)
                            wait(act, dn_done, layer, b, f - 1)
                            act.copy(hs[:, f % 2, 0, :], hb[:, f % 2, :]).then_inc(h_hi.handle, 1)

            walk(act, step)

        @block.vector
        def _(dve):
            prime(dve, "DVE")
            for n, (t, v) in enumerate(((vaug, 1.0), (comb, 0.0), (negh, -0.5))):
                dve.memset(t[tuple(slice(None) for _ in t.shape)], v).then_inc(const_set, 1)
            dve.memset(stkf[:, 1, :, :], 1.0).then_inc(const_set, 1)
            dve.wait_ge(const_loaded, 16 * N_CONST)
            dve.tensor_copy(identb[:, :], ident[:, :]).then_inc(const_set, 1)
            dve.tensor_copy(maskb[:, :, :].rearrange("p a b -> p (a b)"), th[:, 0, :]).then_inc(const_set, 1)

            def ln_stats_of(nl, nb, m):
                dve.wait_ge(x_loaded[m], loaded_by(nl, nb, m))
                for blk in range(BLK):
                    dve.bn_stats(stats[:, blk, :], xt[:, m, blk, :]).then_inc(ln_stats.handle, 1)
                wait(dve, ln_stats, nl, nb, 2)
                alone(dve, dve_passed)
                for blk in range(BLK):
                    dve.bn_aggr(mv[:, blk, :], stats[:, blk, :]).then_inc(ln_stats.handle, 1)

            def normalise(nl, nb, m):
                wait(dve, ln_rstd, nl, nb, 2)
                for blk in range(BLK):
                    last = dve.tensor_scalar(xn[:, blk, :], xt[:, m, blk, :], mv[:, blk, 0:1], rstd[:, blk:blk + 1],
                                             ALU.subtract, ALU.mult)
                last.then_inc(xn_done.handle, 1)

            def x_unit(nl, nb):
                wait(dve, x_hi, nl, nb, 1)
                dve.tensor_tensor(xT[:, 1, :, :].rearrange("p a b -> p (a b)"), banks(nl, "X")[:, 0, :],
                                  xT[:, 0, :, :].rearrange("p a b -> p (a b)").bitcast(F32), ALU.subtract)\
                    .then_inc(read_out(nl, "X"), 1)

            ln_stats_of(0, 0, 0)
            normalise(0, 0, 0)
            dve.wait_ge(w0_hi, 2)
            dve.tensor_tensor(wB[:, 1, :], big[:, 0:N_QKV], wB[:, 0, :].bitcast(F32), ALU.subtract).then_inc(w0_lo, 1)
            dve.tensor_tensor(wA[:, 1, N_GU0:], big[:, N_QKV:N_QKV + N_WO], wA[:, 0, N_GU0:].bitcast(F32),
                              ALU.subtract).then_inc(w0_lo, 1)
            x_unit(0, 0)
            dve.wait_ge(const_hi, 1)
            for c, (w, at, n) in enumerate(LUT_PIECES):
                idx, term, total = idx_slot(c, n), flat(prob, n), flat(pvT, n)
                dve.wait_ge(idx_loaded[c % 2], 16 * (c // 2 + 1))
                dve.wait_ge(w0_lo, 2 + c)
                for k in range(LUT):
                    dve.tensor_scalar(total if k == 0 else term, idx, float(k), lut[:, k:k + 1], ALU.is_equal,
                                      ALU.mult).then_inc(lut_step, 1)
                    dve.wait_ge(lut_step, 2 * LUT * c + 2 * k + 1)
                    if k == 0:
                        dve.memset(term[:, 0:1], 0.0).then_inc(lut_step, 1)
                    else:
                        dve.tensor_tensor(total, total, term, ALU.add).then_inc(lut_step, 1)
                    dve.wait_ge(lut_step, 2 * LUT * c + 2 * k + 2)
                dve.wait_ge(w0_hi, 3 + c)
                dve.tensor_tensor(store(w)[:, 1, at:at + n], total, store(w)[:, 0, at:at + n].bitcast(F32),
                                  ALU.subtract).then_inc(w0_lo, 1)
            dve.sem_inc(raw_lo, 2)

            def late(c0, c1):
                for c in range(c0, c1):
                    w, at, _ = LATE[c]
                    dve.wait_ge(late_hi, c + 1)
                    dve.tensor_tensor(store(w)[:, 1, at:at + LATE_CHUNK], late_slot(c),
                                      store(w)[:, 0, at:at + LATE_CHUNK].bitcast(F32), ALU.subtract).then_inc(late_lo, 1)

            def step(layer, b, n, nxt):
                for s in STEPS[layer]:
                    kind, j = s if isinstance(s, tuple) else (s, None)
                    if kind == "QK" and layer == 0:
                        wait(dve, qk_hi, layer, b, 1)
                        dve.tensor_tensor(split[:, 0:4:3, :, :].rearrange("p a b c -> p a (b c)").bitcast(F32R),
                                          banks(layer, s)[:, :, :],
                                          split[:, 1:3, :, :].rearrange("p a b c -> p a (b c)"), ALU.subtract)\
                            .then_inc(read_out(layer, s), 1)
                    elif kind == "QK":
                        unit_filled(dve, layer, b, s)
                        wait(dve, pv_done, layer, b, 0)
                        dve.tensor_tensor(ropet[:, :, :], banks(layer, s)[:, :, :].rearrange("p a (t s) -> p (a t) s", t=2),
                                          rope[:, 0:1, :].broadcast_to([P, 4, S]), ALU.mult).then_inc(read_out(layer, s), 1)
                    elif kind == "ROT":
                        unit_filled(dve, layer, b, s)
                        wait(dve, stk_loaded, layer, b, 0)
                        for qk in range(2):
                            last = dve.tensor_tensor(split[:, 3 * qk, :, :],
                                                     banks(layer, s)[:, qk, :].rearrange("p (t s) -> p t s", t=2),
                                                     rope[:, 1:2, :].broadcast_to([P, 2, S]), ALU.mult)
                        last.then_inc(read_out(layer, s), 1)
                        wait(dve, qk_hi, layer, b, 1)
                        dve.tensor_tensor(split[:, 0:4:3, :, :].rearrange("p a b c -> p a (b c)").bitcast(F32R),
                                          ropet[:, :, :].rearrange("p (a t) s -> p a (t s)", t=2),
                                          split[:, 1:3, :, :].rearrange("p a b c -> p a (b c)"), ALU.subtract)\
                            .then_inc(qk_lo.handle, 1)
                    elif kind == "LNS" and nxt is not None:
                        ln_stats_of(*nxt)
                    elif kind == "LNN" and nxt is not None:
                        normalise(*nxt)
                    elif kind == "X" and nxt is not None:
                        x_unit(nxt[0], nxt[1])
                        if last_of_layer0(layer, b):
                            late(N_LATE_B, len(LATE) - 1)
                    elif kind == "LT":
                        unit_filled(dve, layer, b, s)
                        dve.tensor_copy(lg[:, :, :], banks(layer, s)[:, 0, 0:BLK * NE].rearrange("p (k e) -> p k e", k=BLK))\
                            .then_inc(read_out(layer, s), 1)
                        unit_read(dve, layer, b, s)
                        alone(dve, dve_passed)
                        for blk in range(BLK):
                            dve.max(m8[:, blk, :], lg[:, blk, :]).then_inc(top_step.handle, 1)
                        wait(dve, top_step, layer, b, 2)
                        alone(dve, dve_passed)
                        for blk in range(BLK):
                            dve.max_index(i8[:, blk, :], m8[:, blk, :], lg[:, blk, :]).then_inc(top_step.handle, 1)
                        dve.tensor_scalar(nmax[:, :], m8[:, :, 0], -1.0, None, ALU.mult).then_inc(top_step.handle, 1)
                        wait(dve, top_step, layer, b, 4)
                        dve.tensor_copy(i8f[:, :, :], i8[:, :, :]).then_inc(top_step.handle, 1)
                        wait(dve, top_step, layer, b, 6)
                        for blk in range(BLK):
                            dve.tensor_scalar(sel0[:, blk, :], iota[:, :], i8f[:, blk, 0:1], None, ALU.is_equal)\
                                .then_inc(top_step.handle, 1)
                        wait(dve, top_step, layer, b, 8)
                        for blk in range(BLK):
                            dve.scalar_tensor_tensor(sel1[:, blk, :], iota[:, :], i8f[:, blk, 1:2], sel0[:, blk, :],
                                                     ALU.is_equal, ALU.add).then_inc(top_step.handle, 1)
                        wait(dve, exps_done, layer, b, 2)
                        dve.reciprocal(rsum[:, :], esum[:, :]).then_inc(top_step.handle, 1)
                        wait(dve, top_step, layer, b, 11)
                        for blk in range(BLK):
                            for at in (0, 32):
                                dve.scalar_tensor_tensor(comb[:, blk, at:at + NE], ex[:, blk, :], rsum[:, blk:blk + 1],
                                                         sel1[:, blk, :], ALU.mult, ALU.mult).then_inc(comb_done.handle, 1)
                    elif kind == "CT":
                        wait(dve, comb_hi, layer, b, 1)
                        dve.tensor_tensor(combT[32:40, :], banks(layer, s)[32:40, 0, 0:S], combT[32:40, :].bitcast(F32),
                                          ALU.subtract).then_inc(read_out(layer, s), 1)
                    elif kind == "MAX":
                        unit_filled(dve, layer, b, s)
                        heads = slice(j, H, NPAIR)
                        dve.tensor_reduce(mx[:, 0, heads], banks(layer, s)[:, :, 0:P], AX.X, ALU.max)
                        dve.tensor_reduce(mx[:, 1, heads], banks(layer, s)[:, :, S:2 * S], AX.X, ALU.max)\
                            .then_inc(read_out(layer, s), 1)
                    elif kind == "NM":
                        if layer == 0:
                            dve.wait_ge(raw_hi, b + 1)
                            dve.tensor_tensor(wD[:, 1, bass.ds(b * STREAM_CHUNK, STREAM_CHUNK)],
                                              big[:, n * SLOT:n * SLOT + STREAM_CHUNK],
                                              wD[:, 0, bass.ds(b * STREAM_CHUNK, STREAM_CHUNK)].bitcast(F32),
                                              ALU.subtract).then_inc(raw_lo, 1)
                        if last_of_layer0(layer, b):
                            late(0, N_LATE_B)
                    elif kind == "ST":
                        if j >= 2 and j % 2 == 0:
                            g = j // 2 - 1
                            wait(dve, pv_done, layer, b, j)
                            dve.tensor_copy(pvT[:, g, :], pv[:, 0, :]).then_inc(pv_out.handle, 1)
                    elif kind == "TR":
                        unit_filled(dve, layer, b, s)
                        heads = banks(layer, s)[:, :, :].rearrange("p k (h d) -> p k h d", d=2 * HD)
                        dve.reciprocal(rden[:, :, :], heads[:, :, :, HD]).then_inc(den_done.handle, 1)
                        wait(dve, den_done, layer, b, 1)
                        dve.tensor_tensor(o_tok.rearrange("p k (h d) -> p k h d", h=H), heads[:, :, :, 0:HD],
                                          rden[:, :, :].unsqueeze(3).broadcast_to([P, BLK, H, HD]), ALU.mult)\
                            .then_inc(read_out(layer, s), 1)
                    elif kind == "OT":
                        wait(dve, o_hi, layer, b, 1)
                        dve.tensor_tensor(oT[:, 1, :, :].rearrange("p a b -> p (a b)"), banks(layer, s)[:, 0, :],
                                          oT[:, 0, :, :].rearrange("p a b -> p (a b)").bitcast(F32), ALU.subtract)\
                            .then_inc(read_out(layer, s), 1)
                    elif kind == "PROJ":
                        wait(dve, acc_ready, layer, b, 1)
                        dve.tensor_tensor(xt[:, n, :, :], acc[:, :, :], xt[:, n, :, :], ALU.add).then_inc(y_done.handle, 1)
                        if last_of_layer0(layer, b):
                            late(len(LATE) - 1, len(LATE))
                    elif kind == "F":
                        if j < NF[layer]:
                            wait(dve, tanh_done, layer, b, j + 1)
                            dve.scalar_tensor_tensor(ga[:, j % 2, :], th[:, j % 2, :], 1.0, gu[j % 2][:, 0, :], ALU.add, ALU.mult)\
                                .then_inc(gate_done.handle, 1)
                        if 1 <= j <= NF[layer]:
                            f = j - 1
                            wait(dve, h_hi, layer, b, f + 1)
                            dve.tensor_tensor(hs[:, f % 2, 1, :], hb[:, f % 2, :], hs[:, f % 2, 0, :].bitcast(F32),
                                              ALU.subtract).then_inc(h_lo.handle, 1)
                        if j < NF[layer]:
                            wait(dve, gate_done, layer, b, j + 1)
                            dve.scalar_tensor_tensor(hb[:, j % 2, :], ga[:, j % 2, :], 0.5, gu[j % 2][:, 1, :], ALU.mult,
                                                     ALU.mult).then_inc(hid_done.handle, 1)

            walk(dve, step)

        @block.gpsimd
        def _(pool):
            prime(pool, "POOL")
            pool.wait_ge(const_set, N_CONST_SET)

            def rstd_of(nl, nb):
                wait(pool, ln_stats, nl, nb, 4)
                alone(pool, pool_passed)
                pool.tensor_scalar(vareps[:, :], mv[:, :, 1], EPS, None, ALU.add).then_inc(ln_rstd.handle, 1)
                wait(pool, ln_rstd, nl, nb, 1)
                pool.tensor_tensor(rstd[:, :], vareps[:, :], negh[:, :], ALU.pow).then_inc(ln_rstd.handle, 1)

            rstd_of(0, 0)

            def step(layer, b, n, nxt):
                for s in STEPS[layer]:
                    kind, j = s if isinstance(s, tuple) else (s, None)
                    if kind == "ROT":
                        unit_read(pool, layer, b, s)
                        for qk in range(2):
                            last = pool.tensor_tensor(ropet[:, 2 * qk:2 * qk + 2, :], ropet[:, 2 * qk:2 * qk + 2, :],
                                                      split[:, 3 * qk, :, :], ALU.add)
                        last.then_inc(rope_sum.handle, 1)
                    elif kind == "LNS" and nxt is not None:
                        rstd_of(nxt[0], nxt[1])
                    elif kind == "ST" and j < NPAIR:
                        unit_read(pool, layer, b, s)
                        alone(pool, pool_passed)
                        diag = prob[:, j % 2, 0:2, :, :].rearrange("p a r c -> p (a r) c")
                        pool.affine_select(out=diag, in_=diag, compare_op=ALU.is_ge, fill=0.0, base=0,
                                           pattern=[[0, 4], [1, P]], channel_multiplier=-1)\
                            .then_inc(masked.handle, 1)
                    elif kind == "F" and layer == 1 and TS <= j < NF[1]:
                        wait(pool, hid_done, layer, b, j + 1)
                        if j == TS:
                            unit_read(pool, layer, b, "CB2")
                            unit_read(pool, layer, b, "CB1")
                        pool.tensor_tensor(hb[:, j % 2, :], hb[:, j % 2, :], combB[:, j - TS, :], ALU.mult)\
                            .then_inc(weighted.handle, 1)

            walk(pool, step)


def layout(a):
    f = np.float32
    order = np.array([(4 * jj + 2 * t + r) * HD + d for t in range(2) for jj in range(4) for r in range(2)
                      for d in range(HD)])
    rot = np.array([(o // HD) * HD + (o % HD + HD // 2) % HD for o in order])

    def rows(w):
        return np.ascontiguousarray(w.reshape(-1, P, w.shape[1]).transpose(1, 0, 2)).reshape(P, -1)

    def padded(w, n, fill=0):
        out = np.full((n,) + w.shape[1:], fill, w.dtype)
        out[:w.shape[0]] = w
        return out

    def gate_up(g, u):
        w = np.stack([g.reshape(-1, P, KT, P), u.reshape(-1, P, KT, P)])
        return np.ascontiguousarray(w.transpose(4, 1, 3, 0, 2)).reshape(P, -1)

    wqkv = a["L0_attn_W_qkv"]
    qkv0 = np.concatenate([wqkv[0:D][order], wqkv[D:2 * D][order], wqkv[2 * D:]]).T
    w0_lin = np.concatenate([rows(qkv0), rows(a["L0_attn_W_proj"].T)], axis=1)
    gi, ui, di = a["L0_ffn_gate_idx"], a["L0_ffn_up_idx"], a["L0_ffn_down_idx"]
    idx0 = np.concatenate([gate_up(padded(gi, T0 * P, LUT), padded(ui, T0 * P, LUT)),
                           rows(padded(np.ascontiguousarray(di.T), T0 * P, LUT))], axis=1)
    wq, wk, wv = a["L1_attn_Wq"], a["L1_attn_Wk"], a["L1_attn_Wv"]
    g1 = np.concatenate([padded(a["L1_ffn_sw1"], TS * P), a["L1_ffn_w1"].reshape(NE * EI, D)])
    u1 = np.concatenate([padded(a["L1_ffn_sw2"], TS * P), a["L1_ffn_w2"].reshape(NE * EI, D)])
    w1_stream = np.concatenate([rows(np.concatenate([wq[order], wk[order], wv]).T),
                                rows(padded(a["L1_ffn_gate_w"], P).T), gate_up(g1, u1)], axis=1)
    dn1 = np.concatenate([padded(np.ascontiguousarray(a["L1_ffn_sw3"].T), TS * P),
                          a["L1_ffn_w3"].transpose(0, 2, 1).reshape(NE * EI, D)])
    w1_late = np.concatenate([rows(dn1), rows(np.concatenate([wq[rot], wk[rot]]).T), rows(a["L1_attn_Wo"].T)], axis=1)

    inv_freq = 1.0 / 10000.0 ** (np.arange(0, HD, 2, dtype=f) / HD)
    freqs = np.einsum("i,j->ij", np.arange(S, dtype=f), inv_freq)
    emb = np.concatenate((freqs, freqs), axis=-1)
    d = np.arange(P) % HD
    sign = np.where(d < HD // 2, -1.0, 1.0).astype(f)[:, None]
    rope = np.stack([np.cos(emb).astype(f).T[d], np.sin(emb).astype(f).T[d] * sign], axis=1)
    q, k = np.arange(P)[:, None], np.arange(P)[None, :]
    mask = np.where(k > q, -1e30, 0.0).astype(f)
    owner = (np.arange(TE * P) // EI)[None, :]
    e = np.arange(64)[:, None]
    esel = (((e < NE) & (e == owner)) | ((e >= 32) & (e - 32 == owner))).astype(f)
    return {
        "x_in": a["L0_attn_x"], "w0_lin": w0_lin, "idx0": idx0, "lut_in": a["L0_ffn_lut"], "w1_stream": w1_stream,
        "w1_late": w1_late, "rope_in": rope.astype(f), "ident_in": np.eye(P, dtype=f),
        "mask_in": np.stack([mask, mask], axis=1).reshape(P, 2 * P), "esel_in": esel,
        "iota_in": np.tile(np.arange(NE, dtype=f), (P, 1)),
    }


def kernel(**inputs):
    import concourse.bacc as bacc
    from concourse.bass_utils import run_bass_kernel_spmd

    arrays = {n: np.ascontiguousarray(v) for n, v in layout({k: np.asarray(v) for k, v in inputs.items()}).items()}
    nc = bacc.Bacc("TRN2", target_bir_lowering=False, num_devices=1)
    args = {n: nc.dram_tensor(n, v.shape, mybir.dt.from_np(v.dtype), kind="ExternalInput").ap()
            for n, v in arrays.items()}
    y = nc.dram_tensor("y_out", (B, S, D), F32, kind="ExternalOutput").ap()
    build(nc, y_out=y, **args)
    r = run_bass_kernel_spmd(nc, [arrays], core_ids=[0])
    return r.results[0]["y_out"]
```

```python
from contextlib import ExitStack

import numpy as np

import concourse.bass as bass
from concourse import mybir

F32 = mybir.dt.float32
F32R = mybir.dt.float32r
BF16 = mybir.dt.bfloat16
I32 = mybir.dt.int32
U32 = mybir.dt.uint32
ALU = mybir.AluOpType
ACT = mybir.ActivationFunctionType
AX = mybir.AxisListType

P = 128
B = 16
S = 256
D = 256
KT = D // P
BLK = S // P
H = 16
HD = D // H
NPAIR = H // 2
LUT = 16
INTER = 688
NE = 8
EI = 176
SI = 352
T0 = -(-INTER // P)
TS = -(-SI // P)
TE = NE * EI // P
NF = (T0, TS + TE)
SCALE = (1.0 / 16.0, 1.0 / 4.0)
EPS = 1e-5

GU_TILE = KT * 2 * P
N_GU0, N_DN0 = T0 * GU_TILE, T0 * D
N_GU1, N_DN1 = NF[1] * GU_TILE, NF[1] * D
N_QKV, N_WO, N_ROT, N_RT = KT * 3 * D, KT * D, KT * 2 * D, KT * P
N_STREAM = N_QKV + N_RT + N_GU1
STREAM_CHUNK = N_STREAM // B
LATE_CHUNK = 512
SLOT = STREAM_CHUNK
N_SLOTS = 5

LUT_PIECE = 1024
LUT_PIECES = [("A", 0, 1024), ("A", 1024, 1024), ("A", 2048, 1024), ("C", 0, 1024), ("C", 1024, 512)]
LATE = [("B", c, N_DN1 + c) for c in range(0, N_QKV, LATE_CHUNK)] \
    + [("A", c, c) for c in range(0, N_GU0, LATE_CHUNK)] + [("A", N_GU0, N_GU0)]
N_LATE_B = N_QKV // LATE_CHUNK
LATE_SLOTS = 3
N_CONST, N_CONST_SET = 6, 6


def late_for_dn(f):
    return N_LATE_B + (f * D) // LATE_CHUNK + 1


PREV = ("NM", "ST", "PV", "TR", "OT", "PROJ", "DP")
NEXT = ("LNS", "LNN")


def steps_of(kind):
    return lambda *js: [(kind, j) for j in js]


ST, STK, PV, MAX, G, H_, D_, DP = (steps_of(kind) for kind in ("ST", "STK", "PV", "MAX", "G", "H", "D", "DP"))


def tiles(j0, j1):
    return [s for j in range(j0, j1) for s in (("G", j), ("H", j - 1), ("D", j - 2))]


STEPS = (
    ["X"] + DP(0) + ["NM"] + DP(1) + ["QK"] + ST(0, 1) + STK(0) + G(0) + ST(2, 3) + STK(1) + H_(0)
    + PV(0) + G(1) + ST(4, 5) + STK(2) + H_(1) + PV(1) + ST(6, 7) + STK(3) + PV(2) + G(2) + MAX(0) + PV(3)
    + ["V", "TR"] + MAX(1) + G(3) + ["OT"] + MAX(2) + ["PROJ"] + MAX(3) + D_(0) + H_(2) + D_(1) + H_(3) + ["RAW"]
    + MAX(4) + G(4) + D_(2) + ["LNS"] + MAX(5) + G(5) + D_(3) + H_(4) + ["LNN"] + MAX(6, 7) + H_(5) + ["LATE"],
    ["X"] + DP(0) + ["NM"] + DP(1) + ["QK", "ROT"] + ST(0, 1) + ["ROTLO"] + STK(0) + G(0) + ST(2, 3)
    + STK(1) + H_(0) + PV(0) + G(1) + ST(4, 5) + STK(2) + H_(1) + PV(1) + ST(6, 7) + STK(3) + PV(2) + G(2)
    + MAX(0) + PV(3) + ["VR", "TR"] + MAX(1) + ["OT", "LT"] + MAX(2) + ["PROJ"] + MAX(3) + D_(0) + H_(2) + D_(1)
    + ["CT"] + MAX(4) + ["CB0"] + G(3) + D_(2) + ["CB1"] + G(4) + H_(3) + MAX(5) + ["CB2"] + tiles(5, 6) + ["LNS"]
    + MAX(6) + tiles(6, 8) + ["LNN"] + MAX(7) + tiles(8, NF[1]) + H_(NF[1] - 1),
)
UNIT_KINDS = ("X", "NM", "QK", "ROT", "TR", "V", "VR", "OT", "LT", "CT", "CB0", "CB1", "CB2", "MAX")
UNITS = [[u for u in steps if (u[0] if isinstance(u, tuple) else u) in UNIT_KINDS or (u[0] == "ST" and u[1] < NPAIR)]
         for steps in STEPS]
assert all(len(u) % 2 == 0 for u in UNITS)

CREDIT = 3


class Counter:

    def __init__(self, handle, per, by=1):
        self.handle, self.per, self.by = handle, per, by

    def at(self, layer, b, k):
        if layer == 0:
            return b * (self.per[0] * self.by) + (CREDIT + k) * self.by
        return b * (self.per[1] * self.by) + (CREDIT + B * self.per[0] + k) * self.by


def build(nc, x_in, w0_lin, idx0, lut_in, w1_stream, w1_late, rope_in, ident_in, mask_in, esel_in, iota_in, y_out):
    x1 = nc.dram_tensor("x1_scratch", (B, BLK, P, D), F32, kind="Internal").ap()
    src = (x_in.rearrange("b (k p) d -> b p k d", p=P), x1.rearrange("b k p d -> b p k d"))
    dst = (x1.rearrange("b k p d -> b p k d"), y_out.rearrange("b (k p) d -> b p k d", p=P))

    with ExitStack() as ctx:
        def sb(name, shape, dt=F32):
            return ctx.enter_context(nc.sbuf_tensor(name, shape, dt))

        counters = []

        def counter(name, per, by=1):
            c = Counter(ctx.enter_context(nc.semaphore(name)), per, by)
            counters.append(c)
            return c

        def sem(name):
            return ctx.enter_context(nc.semaphore(name))

        wA = sb("wA", [P, 2, N_DN1], F32R)
        wB = sb("wB", [P, 2, N_QKV], F32R)
        wD = sb("wD", [P, 2, N_STREAM], F32R)
        assert N_GU0 + N_WO == N_DN1 and N_ROT + N_WO == N_QKV
        GU = (wA[:, :, 0:N_GU0].rearrange("p s (f k g c) -> p s f k g c", f=T0, k=KT, g=2),
              wD[:, :, N_QKV + N_RT:].rearrange("p s (f k g c) -> p s f k g c", f=NF[1], k=KT, g=2))
        QKV = (wB[:, :, :].rearrange("p s (k c) -> p s k c", k=KT), wD[:, :, 0:N_QKV].rearrange("p s (k c) -> p s k c", k=KT))
        WO = (wA[:, :, N_GU0:].rearrange("p s (k c) -> p s k c", k=KT), wB[:, :, N_ROT:].rearrange("p s (k c) -> p s k c", k=KT))
        ROTW = wB[:, :, 0:N_ROT].rearrange("p s (k c) -> p s k c", k=KT)
        RTW = wD[:, :, N_QKV:N_QKV + N_RT].rearrange("p s (k c) -> p s k c", k=KT)

        ident = sb("ident", [P, P])
        identb = sb("identb", [P, P], BF16)
        maskb = sb("maskb", [P, 2, P], BF16)
        rope = sb("rope", [P, 2, S])
        esel = sb("esel", [64, TE, P], F32R)
        iota = sb("iota", [P, NE])
        lut = sb("lut", [P, LUT])
        negh = sb("negh", [P, BLK])

        xt = sb("xt", [P, 2, BLK, D])
        stats = sb("stats", [P, BLK, 6])
        mv = sb("mv", [P, BLK, 2])
        vareps = sb("vareps", [P, BLK])
        rstd = sb("rstd", [P, BLK])
        xn = sb("xn", [P, BLK, D])
        xT = sb("xT", [P, 2, KT, S], F32R)
        split = sb("split", [P, 4, 2, S])
        stk = sb("stk", [P, 2, NPAIR, S], F32R)
        stkf = stk[:, :, :, :].bitcast(F32)
        vaug = sb("vaug", [P, BLK, H, 2 * HD])
        mx = sb("mx", [P, BLK, H])
        nmT = sb("nmT", [H, S])
        nmTr = nmT[:, :].bitcast(F32R)
        prob = sb("prob", [P, 2, 3, 2, P])
        pvT = sb("pvT", [P, 4, S])
        rden = sb("rden", [P, BLK, H])
        o_tok = pvT[:, 0:2, :]
        oT = sb("oT", [P, 2, KT, S], F32R)
        th = sb("th", [P, 2, S])
        ga = sb("ga", [P, 2, S])
        hb = sb("hb", [P, 2, S])
        hs = sb("hs", [P, 2, 2, S], F32R)
        big = sb("big", [P, N_SLOTS * SLOT + 16])
        combB = big[:, 0:TE * S].rearrange("p (t s) -> p t s", t=TE)
        ropet = pvT[:, :, :]
        lgT = nmT[0:NE, :]
        lg = sb("lg", [P, BLK, NE])
        m8 = sb("m8", [P, BLK, 8])
        i8 = sb("i8", [P, BLK, 8], U32)
        i8f = sb("i8f", [P, BLK, 8])
        nmax = sb("nmax", [P, BLK])
        ex = sb("ex", [P, BLK, NE])
        esum = sb("esum", [P, BLK])
        rsum = sb("rsum", [P, BLK])
        sel0 = sb("sel0", [P, BLK, NE])
        sel1 = sb("sel1", [P, BLK, NE])
        comb = sb("comb", [P, BLK, 40])
        combT = sb("combT", [40, S], F32R)

        with nc.sbuf_tensor("wC", [P, 2, N_DN0], F32R) as wC:
            pass
        probx = sb("probx", [P, 12 * P])
        DN = (wC[:, :, :].rearrange("p s (f c) -> p s f c", f=T0), wA[:, :, :].rearrange("p s (f c) -> p s f c", f=NF[1]))

        pair = [ctx.enter_context(nc.psum_tensor(f"pair{n}", [P, 2, 512], F32)) for n in "ab"]
        pv = ctx.enter_context(nc.psum_tensor("pv", [P, 2, S], F32))
        acc = ctx.enter_context(nc.psum_tensor("acc", [P, BLK, D], F32))
        gu = [ctx.enter_context(nc.psum_tensor(f"gu{n}", [P, 2, S], F32)) for n in range(2)]

        unit_ready = counter("unit_ready", (len(UNITS[0]), len(UNITS[1])))
        pair_done = [counter(f"pair_done_{n}", (len(UNITS[0]) // 2, len(UNITS[1]) // 2)) for n in "ab"]
        ln_stats = counter("ln_stats", (4, 4))
        ln_rstd = counter("ln_rstd", (2, 2))
        xn_done = counter("xn_done", (1, 1))
        x_hi = counter("x_hi", (1, 1))
        qk_hi = counter("qk_hi", (1, 1))
        qk_lo = counter("qk_lo", (0, 1))
        rope_sum = counter("rope_sum", (0, 1))
        stk_loaded = [counter(f"stk_loaded{n}", (6, 6), 16) for n in range(4)]
        nm_loaded = counter("nm_loaded", (2, 2), 16)
        masked = counter("masked", (8, 8))
        pv_done = counter("pv_done", (4, 4))
        pv_out = counter("pv_out", (4, 4))
        den_done = counter("den_done", (1, 1))
        o_hi = counter("o_hi", (1, 1))
        gu_ready = counter("gu_ready", NF)
        tanh_done = counter("tanh_done", NF)
        gate_done = counter("gate_done", NF)
        hid_done = counter("hid_done", NF)
        weighted = counter("weighted", (0, TE))
        h_hi = counter("h_hi", NF)
        h_lo = counter("h_lo", NF)
        dn_done = counter("dn_done", NF)
        acc_ready = counter("acc_ready", (1, 1))
        y_done = counter("y_done", (1, 1))
        top_step = counter("top_step", (0, 11))
        exps_done = counter("exps_done", (0, 2))
        comb_done = counter("comb_done", (0, 4))
        comb_hi = counter("comb_hi", (0, 1))
        MADE_BY = {
            "PE": (unit_ready, pv_done, gu_ready, dn_done, acc_ready),
            "ACT": (x_hi, qk_hi, o_hi, tanh_done, h_hi, exps_done, comb_hi),
            "DVE": (pair_done[0], pair_done[1], ln_stats, xn_done, qk_lo, pv_out, den_done, gate_done, hid_done,
                    h_lo, y_done, top_step, comb_done),
            "POOL": (ln_rstd, rope_sum, masked, weighted),
            "SP": (*stk_loaded, nm_loaded),
        }
        assert sorted(id(c) for v in MADE_BY.values() for c in v) == sorted(id(c) for c in counters)
        x_loaded = [sem(f"x_loaded{n}") for n in range(2)]
        y_stored = [sem(f"y_stored{n}") for n in range(2)]
        raw_loaded = [sem(f"raw_loaded{n}") for n in range(2)]
        raw_hi, raw_lo = sem("raw_hi"), sem("raw_lo")
        late_loaded = [sem(f"late_loaded{n}") for n in range(LATE_SLOTS)]
        late_hi, late_lo = sem("late_hi"), sem("late_lo")
        const_loaded, const_hi, const_set = sem("const_loaded"), sem("const_hi"), sem("const_set")
        w0_loaded, w0_hi, w0_lo = sem("w0_loaded"), sem("w0_hi"), sem("w0_lo")
        idx_loaded = [sem(f"idx_loaded{n}") for n in range(2)]
        lut_step = sem("lut_step")
        dve_passed, pool_passed, sp_passed = sem("dve_passed"), sem("pool_passed"), sem("sp_passed")

        def prime(eng, who):
            for c in MADE_BY[who]:
                eng.sem_inc(c.handle, CREDIT * c.by)

        def wait(eng, c, layer, b, k):
            eng.wait_ge(c.handle, c.at(layer, b, k))

        def alone(eng, passed):
            eng.sem_inc(passed, 1)

        def unit(layer, what):
            j = UNITS[layer].index(what)
            return j, j % 2, j // 2

        def unit_filled(eng, rnd, what):
            wait(eng, unit_ready, *rnd, unit(rnd[0], what)[0] + 1)

        def unit_read(eng, rnd, what):
            _, p, turn = unit(rnd[0], what)
            wait(eng, pair_done[p], *rnd, turn + 1)

        def banks_free(eng, rnd, what):
            _, p, turn = unit(rnd[0], what)
            wait(eng, pair_done[p], *rnd, turn)

        def banks(rnd, what):
            return pair[unit(rnd[0], what)[1]]

        def read_out(rnd, what):
            return pair_done[unit(rnd[0], what)[1]].handle

        def stored_two_before(layer, b, n):
            return (b - n) * (16 // 2) + 16 * (1 + layer * (B // 2))

        def loaded_by(layer, b, n):
            return (b - n) * (16 // 2) + 16 * (1 + layer * (B // 2))

        def walk(eng, step, left_out=None):
            def go(rnd, prev, own, nxt):
                for s in STEPS[rnd[0]]:
                    kind, j = s if isinstance(s, tuple) else (s, None)
                    batch = prev if kind in PREV else nxt if kind in NEXT else own
                    if batch is not None:
                        step(rnd, s, kind, j, batch)
                    elif left_out is not None and s in UNITS[rnd[0]]:
                        left_out(rnd, s)

            for layer in range(2):
                go((layer, 0), (0, B - 1, 1) if layer else None, (layer, 0, 0), (layer, 1, 1))
                with eng.Fori(0, B // 2 - 1) as i:
                    for n in (1, 0):
                        b = i * 2 + (2 - n)
                        go((layer, b), (layer, b - 1, 1 - n), (layer, b, n), (layer, b + 1, 1 - n))
                go((layer, B - 1), (layer, B - 2, 0), (layer, B - 1, 1), None if layer else (1, 0, 0))
            go((1, B), (1, B - 1, 1), None, None)

        def last_of_layer0(layer, b):
            return layer == 0 and isinstance(b, int) and b == B - 1

        def prob_of(layer, u):
            if u % 4 < 2:
                return prob[:, u % 4]
            return (big[:, 2 * SLOT:2 * SLOT + 12 * P] if layer == 0 else probx[:, :])\
                .rearrange("p (u a r c) -> p u a r c", u=2, a=3, r=2)[:, u % 2]

        def dram_batch(view, b):
            return view[bass.ds(b, 1)].rearrange("a p k d -> (a p) k d")

        def flat(t, n, dt=None):
            dims = " ".join("abcde"[:len(t.shape) - 1])
            v = t[tuple(slice(None) for _ in t.shape)]
            v = v.rearrange(f"p {dims} -> p ({dims})") if len(t.shape) > 2 else v
            v = v[:, 0:n]
            return v.bitcast(dt) if dt is not None else v

        def store(w):
            return {"A": wA, "B": wB, "C": wC}[w]

        def late_slot(c):
            s = 2 + c % LATE_SLOTS
            return big[:, s * SLOT:s * SLOT + LATE_CHUNK]

        def idx_slot(c, n):
            return flat(split, 2048, I32)[:, (c % 2) * LUT_PIECE:(c % 2) * LUT_PIECE + n]

        block = ctx.enter_context(nc.Block())

        @block.sync
        def _(sp):
            prime(sp, "SP")
            for n in range(2):
                sp.sem_inc(y_stored[n], 16)
            sp.dma_start(xt[:, 0, :, :], dram_batch(src[0], 0)).then_inc(x_loaded[0], 16)
            sp.dma_start(lut[:, :], lut_in.partition_broadcast(P)).then_inc(const_loaded, 16)
            sp.dma_start(ident[:, :], ident_in).then_inc(const_loaded, 16)
            sp.dma_start(th[:, 0, :], mask_in).then_inc(const_loaded, 16)
            sp.dma_start(rope[:, :, :], rope_in).then_inc(const_loaded, 16)
            sp.dma_start(iota[:, :], iota_in).then_inc(const_loaded, 16)
            sp.dma_start(flat(prob, TE * P)[0:64], esel_in).then_inc(const_loaded, 16)
            for c, (_, _, n) in enumerate(LUT_PIECES):
                if c >= 2:
                    sp.wait_ge(lut_step, 2 * LUT * (c - 1))
                sp.dma_start(idx_slot(c, n), idx0[:, c * LUT_PIECE:c * LUT_PIECE + n]).then_inc(idx_loaded[c % 2], 16)
                if c == 1:
                    sp.dma_start(big[:, 0:N_QKV], w0_lin[:, 0:N_QKV]).then_inc(w0_loaded, 16)
                    sp.dma_start(big[:, N_QKV:N_QKV + N_WO], w0_lin[:, N_QKV:]).then_inc(w0_loaded, 16)
            sp.wait_ge(w0_lo, 2 + len(LUT_PIECES))

            def stack_rows(jj):
                for r in range(2):
                    p0 = 32 * jj + 16 * r
                    for c, parts in enumerate((slice(1, 3), slice(0, 3, 2), slice(1, 4, 2))):
                        q0 = 64 * r + 16 * c
                        sp.dma_start(stkf[q0:q0 + 16, :, 2 * jj:2 * jj + 2, :], split[p0:p0 + 16, parts, :, :])\
                            .then_inc(stk_loaded[jj].handle, 16)

            def load_x(layer, b, n):
                sp.wait_ge(y_stored[n], stored_two_before(layer, b, n))
                alone(sp, sp_passed)
                sp.dma_start(xt[:, n, :, :], dram_batch(src[layer], b)).then_inc(x_loaded[n], 16)

            def step(rnd, s, kind, j, batch):
                layer, b, n = batch
                if kind == "NM":
                    unit_read(sp, rnd, s)
                    for r in range(2):
                        sp.dma_start(stkf[64 * r + 48:64 * r + 49, 0, :, :], nmT[8 * r:8 * r + 8, :])\
                            .then_inc(nm_loaded.handle, 16)
                elif kind == "STK":
                    if j == 0:
                        if layer == 0:
                            unit_read(sp, rnd, "QK")
                        else:
                            wait(sp, qk_lo, layer, b, 1)
                        alone(sp, sp_passed)
                    unit_filled(sp, rnd, ("ST", 2 * j + 1))
                    stack_rows(j)
                elif kind == "RAW":
                    sp.wait_ge(raw_lo, b + 1)
                    alone(sp, sp_passed)
                    sp.dma_start(big[:, n * SLOT:n * SLOT + STREAM_CHUNK],
                                 w1_stream[:, bass.ds(b * STREAM_CHUNK, STREAM_CHUNK)])\
                        .then_inc(raw_loaded[n], 16)
                    if last_of_layer0(layer, b):
                        wait(sp, pv_done, 0, b - 1, 4)
                        for c in range(LATE_SLOTS):
                            sp.dma_start(late_slot(c), w1_late[:, LATE[c][2]:LATE[c][2] + LATE_CHUNK])\
                                .then_inc(late_loaded[c % LATE_SLOTS], 16)
                elif kind == "LATE" and last_of_layer0(layer, b):
                    for c in range(LATE_SLOTS, len(LATE)):
                        sp.wait_ge(late_lo, c - LATE_SLOTS + 1)
                        sp.dma_start(late_slot(c), w1_late[:, LATE[c][2]:LATE[c][2] + LATE_CHUNK])\
                            .then_inc(late_loaded[c % LATE_SLOTS], 16)
                elif kind == "PROJ":
                    wait(sp, y_done, layer, b, 1)
                    alone(sp, sp_passed)
                    sp.dma_start(dram_batch(dst[layer], b), xt[:, n, :, :]).then_inc(y_stored[n], 16)
                elif kind == "LNS":
                    load_x(layer, b, n)

            walk(sp, step)
            for n in range(2):
                sp.wait_ge(y_stored[n], 16 * (1 + B))

        @block.tensor
        def _(pe):
            prime(pe, "PE")

            def three(out, lhs, rhs, start, stop=False, **more):
                pe.matmul(out, lhs(0), rhs(0), start=start, stop=False, **more)
                pe.matmul(out, lhs(0), rhs(1), start=False, stop=False, **more)
                return pe.matmul(out, lhs(1), rhs(0), start=False, stop=stop, **more)

            def left_out(rnd, s):
                wait(pe, unit_ready, *rnd, unit(rnd[0], s)[0])
                banks_free(pe, rnd, s)
                pe.sem_inc(unit_ready.handle, 1)
                pe.sem_inc(read_out(rnd, s), 1)

            pe.wait_ge(const_loaded, 16 * N_CONST)
            pe.wait_ge(const_set, N_CONST_SET)
            pe.wait_ge(const_hi, 1)
            pe.wait_ge(w0_lo, 2 + len(LUT_PIECES))

            def step(rnd, s, kind, j, batch):
                layer, b, n = batch
                if kind in ("QK", "ROT"):
                    banks_free(pe, rnd, s)
                    if kind == "QK":
                        unit_read(pe, rnd, "X")
                        if layer == 1:
                            pe.wait_ge(raw_lo, 2 + B)
                    else:
                        pe.wait_ge(late_lo, N_LATE_B)
                    w = QKV[layer] if kind == "QK" else ROTW
                    for qk in range(2):
                        for t in range(2):
                            for kt in range(KT):
                                mm = three(banks(rnd, s)[:, qk, t * S:(t + 1) * S],
                                           lambda h: w[:, h, kt, (2 * qk + t) * P:(2 * qk + t + 1) * P],
                                           lambda h: xT[:, h, kt, :], start=kt == 0, stop=kt == KT - 1)
                    mm.then_inc(unit_ready.handle, 1)
                elif kind in ("V", "VR"):
                    banks_free(pe, rnd, s)
                    for blk in range(BLK):
                        for kt in range(KT):
                            mm = three(banks(rnd, s)[:, 0, blk * D:(blk + 1) * D],
                                       lambda h: xT[:, h, kt, blk * P:(blk + 1) * P],
                                       lambda h: QKV[layer][:, h, kt, 2 * D:3 * D], start=kt == 0, stop=kt == KT - 1)
                    if kind == "VR":
                        for kt in range(KT):
                            mm = three(banks(rnd, s)[:, 1, 0:S], lambda h: RTW[:, h, kt, :],
                                       lambda h: xT[:, h, kt, :], start=kt == 0, stop=kt == KT - 1)
                    mm.then_inc(unit_ready.handle, 1)
                elif kind == "LT":
                    banks_free(pe, rnd, s)
                    unit_read(pe, rnd, "VR")
                    for blk in range(BLK):
                        mm = pe.matmul(banks(rnd, s)[:, 0, blk * NE:(blk + 1) * NE], nmT[0:NE, blk * P:(blk + 1) * P],
                                       ident[0:NE, 0:NE], start=True, stop=True)
                    mm.then_inc(unit_ready.handle, 1)
                elif kind == "CT":
                    banks_free(pe, rnd, s)
                    wait(pe, comb_done, layer, b, 4)
                    for blk in range(BLK):
                        mm = pe.matmul(banks(rnd, s)[0:40, 0, blk * P:(blk + 1) * P], comb[:, blk, :], ident[:, :],
                                       start=True, stop=True)
                    mm.then_inc(unit_ready.handle, 1)
                elif kind in ("CB0", "CB1", "CB2"):
                    banks_free(pe, rnd, s)
                    unit_read(pe, rnd, "CT")
                    c = int(kind[2])
                    for x, t in enumerate(range(4 * c, min(4 * c + 4, TE))):
                        mm = pe.matmul(banks(rnd, s)[:, x // 2, (x % 2) * S:(x % 2 + 1) * S], esel[0:40, t, :],
                                       combT[:, :], start=True, stop=True)
                    mm.then_inc(unit_ready.handle, 1)
                elif kind == "MAX":
                    banks_free(pe, rnd, s)
                    if j % 2 == 0:
                        wait(pe, stk_loaded[j // 2], layer, b, 6)
                    for blk in range(BLK):
                        for r in range(2):
                            rows = slice(64 * r, 64 * r + 48)
                            pe.matmul(banks(rnd, s)[:, r, blk * S:(blk + 1) * S],
                                      stk[rows, 0, j, blk * P:(blk + 1) * P], stk[rows, 1, j, :],
                                      start=blk == 0, stop=False, skip_group_check=True)
                    for r in range(2):
                        diag = banks(rnd, s)[:, r, :].rearrange("p (a c) -> p a c", c=P)[:, 0:4:3, :]
                        mm = pe.matmul(diag, identb[:, :], maskb[:, :, :], start=False, stop=True,
                                       skip_group_check=True)
                    mm.then_inc(unit_ready.handle, 1)
                elif kind == "NM":
                    banks_free(pe, rnd, s)
                    unit_read(pe, (layer, b), ("MAX", NPAIR - 1))
                    for blk in range(BLK):
                        mm = pe.matmul(banks(rnd, s)[0:H, 0, blk * P:(blk + 1) * P], mx[:, blk, :], ident[:, :],
                                       start=True, stop=True)
                    mm.then_inc(unit_ready.handle, 1)
                elif kind == "ST":
                    banks_free(pe, rnd, s)
                    if j == 0:
                        wait(pe, nm_loaded, layer, b, 2)
                    for kb in range(BLK):
                        for r in range(2):
                            rows = slice(64 * r, 64 * r + 49)
                            mm = pe.matmul(banks(rnd, s)[:, r, kb * S:(kb + 1) * S],
                                           stk[rows, 1, j, kb * P:(kb + 1) * P], stk[rows, 0, j, :],
                                           start=True, stop=True)
                    mm.then_inc(unit_ready.handle, 1)
                elif kind == "PV":
                    wait(pe, masked, layer, b, 2 * j + 2)
                    wait(pe, pv_out, layer, b, j)
                    for kb in range(BLK):
                        for x in range(4):
                            u, r, rows = 2 * j + x // 2, x % 2, slice(32 * x, 32 * x + 32)
                            if kb == 0:
                                pe.matmul(pv[rows, 0, :].rearrange("p (a c) -> p a c", a=2), vaug[:, 0, 4 * j + x, :],
                                          prob_of(rnd[0], u)[:, 0:3:2, r, :], start=True, stop=False,
                                          skip_group_check=True)
                            else:
                                mm = pe.matmul(pv[rows, 0, P:S], vaug[:, 1, 4 * j + x, :],
                                               prob_of(rnd[0], u)[:, 1, r, :], start=False, stop=True,
                                               skip_group_check=True)
                    mm.then_inc(pv_done.handle, 1)
                elif kind == "TR":
                    banks_free(pe, rnd, s)
                    wait(pe, pv_out, layer, b, 4)
                    for blk in range(BLK):
                        for g in range(4):
                            mm = pe.transpose(banks(rnd, s)[:, blk, g * P:(g + 1) * P],
                                              pvT[:, g, blk * P:(blk + 1) * P], ident[:, :])
                    mm.then_inc(unit_ready.handle, 1)
                elif kind == "OT":
                    banks_free(pe, rnd, s)
                    unit_read(pe, rnd, "TR")
                    for kt in range(KT):
                        for blk in range(BLK):
                            mm = pe.transpose(banks(rnd, s)[:, 0, kt * S + blk * P:kt * S + (blk + 1) * P],
                                              o_tok[:, blk, kt * P:(kt + 1) * P], ident[:, :])
                    mm.then_inc(unit_ready.handle, 1)
                elif kind == "X":
                    wait(pe, xn_done, layer, b, 1)
                    banks_free(pe, rnd, s)
                    for kt in range(KT):
                        for blk in range(BLK):
                            mm = pe.transpose(banks(rnd, s)[:, 0, kt * S + blk * P:kt * S + (blk + 1) * P],
                                              xn[:, blk, kt * P:(kt + 1) * P], ident[:, :])
                    mm.then_inc(unit_ready.handle, 1)
                elif kind == "PROJ":
                    unit_read(pe, rnd, "OT")
                    for blk in range(BLK):
                        for kt in range(KT):
                            mm = three(acc[:, blk, :], lambda h: oT[:, h, kt, blk * P:(blk + 1) * P],
                                       lambda h: WO[layer][:, h, kt, :], start=False, skip_group_check=True,
                                       stop=blk == BLK - 1 and kt == KT - 1)
                    mm.then_inc(acc_ready.handle, 1)
                elif kind == "G":
                    wait(pe, hid_done, layer, b, j - 1)
                    for g in range(2):
                        for kt in range(KT):
                            mm = three(gu[j % 2][:, g, :], lambda h: GU[layer][:, h, j, kt, g, :],
                                       lambda h: xT[:, h, kt, :], start=kt == 0, stop=kt == KT - 1)
                    mm.then_inc(gu_ready.handle, 1)
                elif kind in ("D", "DP"):
                    if kind == "DP":
                        j += NF[layer] - 2
                    wait(pe, h_lo, layer, b, j + 1)
                    if j == 0:
                        wait(pe, y_done, layer, b, 0)
                    if layer == 1:
                        pe.wait_ge(late_lo, late_for_dn(j))
                    for blk in range(BLK):
                        mm = three(acc[:, blk, :], lambda h: hs[:, j % 2, h, blk * P:(blk + 1) * P],
                                   lambda h: DN[layer][:, h, j, :], start=j == 0 and blk == 0,
                                   skip_group_check=True)
                    mm.then_inc(dn_done.handle, 1)

            walk(pe, step, left_out)

        @block.scalar
        def _(act):
            prime(act, "ACT")
            act.wait_ge(const_loaded, 16 * N_CONST)
            act.copy(esel[:, :, :].rearrange("p a b -> p (a b)"), flat(prob, TE * P)[0:64]).then_inc(const_hi, 1)
            act.wait_ge(w0_loaded, 32)
            act.copy(wB[:, 0, :], big[:, 0:N_QKV]).then_inc(w0_hi, 1)
            act.copy(wA[:, 0, N_GU0:], big[:, N_QKV:N_QKV + N_WO]).then_inc(w0_hi, 1)

            for c, (w, at, n) in enumerate(LUT_PIECES):
                act.wait_ge(lut_step, 2 * LUT * (c + 1))
                act.copy(store(w)[:, 0, at:at + n], flat(pvT, n)).then_inc(w0_hi, 1)

            def late(c0, c1):
                for c in range(c0, c1):
                    w, at, _ = LATE[c]
                    act.wait_ge(late_loaded[c % LATE_SLOTS], 16 * (c // LATE_SLOTS + 1))
                    act.copy(store(w)[:, 0, at:at + LATE_CHUNK], late_slot(c)).then_inc(late_hi, 1)

            def step(rnd, s, kind, j, batch):
                layer, b, n = batch
                if kind == "QK" and layer == 0:
                    unit_filled(act, rnd, s)
                    act.copy(split[:, 1:3, :, :].rearrange("p a b c -> p a (b c)").bitcast(F32R),
                             banks(rnd, s)[:, :, :]).then_inc(qk_hi.handle, 1)
                elif kind == "ROT":
                    wait(act, rope_sum, layer, b, 1)
                    act.copy(split[:, 1:3, :, :].rearrange("p a b c -> p (a b c)").bitcast(F32R),
                             ropet.rearrange("p a s -> p (a s)")).then_inc(qk_hi.handle, 1)
                elif kind in ("V", "VR"):
                    unit_filled(act, rnd, s)
                    v = act.copy(vaug[:, :, :, 0:HD],
                                 banks(rnd, s)[:, 0, :].rearrange("p (k h d) -> p k h d", k=BLK, h=H))
                    if kind == "V":
                        v.then_inc(read_out(rnd, s), 1)
                    else:
                        act.copy(lgT, banks(rnd, s)[0:NE, 1, 0:S]).then_inc(read_out(rnd, s), 1)
                elif kind == "LT":
                    wait(act, top_step, layer, b, 5)
                    for blk in range(BLK):
                        act.activation(ex[:, blk, :], lg[:, blk, :], ACT.Exp, bias=nmax[:, blk:blk + 1],
                                       accum_out=esum[:, blk:blk + 1]).then_inc(exps_done.handle, 1)
                elif kind == "CT":
                    unit_filled(act, rnd, s)
                    act.copy(combT[:, :], banks(rnd, s)[0:40, 0, 0:S]).then_inc(comb_hi.handle, 1)
                elif kind in ("CB0", "CB1", "CB2"):
                    c = int(kind[2])
                    nt = min(4, TE - 4 * c)
                    unit_filled(act, rnd, s)
                    if c == 0:
                        wait(act, weighted, layer, b, 0)
                        act.wait_ge(late_lo, len(LATE))
                    act.copy(combB[:, 4 * c:4 * c + nt, :].rearrange("p a b -> p (a b)"),
                             banks(rnd, s)[:, :, :].rearrange("p a b -> p (a b)")[:, 0:nt * S])\
                        .then_inc(read_out(rnd, s), 1)
                elif kind == "NM":
                    unit_filled(act, rnd, s)
                    act.activation(nmT[:, :].bitcast(F32R), banks(rnd, s)[0:H, 0, 0:S], ACT.Copy, scale=-1.0)\
                        .then_inc(read_out(rnd, s), 1)
                elif kind == "RAW":
                    if last_of_layer0(layer, b):
                        late(0, N_LATE_B)
                elif kind == "ST":
                    unit_filled(act, rnd, s)
                    if j % 2 == 0:
                        wait(act, pv_done, layer, b, j // 2 - 1)
                    act.activation(prob_of(rnd[0], j)[:, 0:3:2].rearrange("p a r c -> p r a c"),
                                   banks(rnd, s)[:, :, 0:S].rearrange("p r (a c) -> p r a c", c=P), ACT.Exp,
                                   scale=SCALE[layer])
                    act.activation(prob_of(rnd[0], j)[:, 1], banks(rnd, s)[:, :, S + P:2 * S], ACT.Exp,
                                   scale=SCALE[layer]).then_inc(read_out(rnd, s), 1)
                elif kind == "OT":
                    unit_filled(act, rnd, s)
                    act.copy(oT[:, 0, :, :].rearrange("p a b -> p (a b)"), banks(rnd, s)[:, 0, :])\
                        .then_inc(o_hi.handle, 1)
                elif kind == "X":
                    unit_filled(act, rnd, s)
                    act.copy(xT[:, 0, :, :].rearrange("p a b -> p (a b)"), banks(rnd, s)[:, 0, :]).then_inc(x_hi.handle, 1)
                elif kind == "LATE":
                    act.wait_ge(raw_loaded[n], (b - n) * 8 + 16)
                    act.copy(wD[:, 0, bass.ds(b * STREAM_CHUNK, STREAM_CHUNK)],
                             big[:, n * SLOT:n * SLOT + STREAM_CHUNK]).then_inc(raw_hi, 1)
                    if last_of_layer0(layer, b):
                        late(N_LATE_B, len(LATE) - 1)
                elif kind == "PROJ" and last_of_layer0(layer, b):
                    wait(act, acc_ready, layer, b, 1)
                    late(len(LATE) - 1, len(LATE))
                elif kind == "G":
                    wait(act, gu_ready, layer, b, j + 1)
                    wait(act, gate_done, layer, b, j - 1)
                    act.activation(th[:, j % 2, :], gu[j % 2][:, 0, :], ACT.Tanh, scale=0.5)\
                        .then_inc(tanh_done.handle, 1)
                elif kind == "H":
                    if layer == 1 and j >= TS:
                        wait(act, weighted, layer, b, j - TS + 1)
                    else:
                        wait(act, hid_done, layer, b, j + 1)
                    wait(act, dn_done, layer, b, j - 1)
                    act.copy(hs[:, j % 2, 0, :], hb[:, j % 2, :]).then_inc(h_hi.handle, 1)

            walk(act, step)

        @block.vector
        def _(dve):
            prime(dve, "DVE")
            for n, (t, v) in enumerate(((vaug, 1.0), (comb, 0.0), (negh, -0.5))):
                dve.memset(t[tuple(slice(None) for _ in t.shape)], v).then_inc(const_set, 1)
            dve.memset(stkf[:, 1, :, :], 1.0).then_inc(const_set, 1)
            dve.wait_ge(const_loaded, 16 * N_CONST)
            dve.tensor_copy(identb[:, :], ident[:, :]).then_inc(const_set, 1)
            dve.tensor_copy(maskb[:, :, :].rearrange("p a b -> p (a b)"), th[:, 0, :]).then_inc(const_set, 1)

            def ln_stats_of(nl, nb, m):
                dve.wait_ge(x_loaded[m], loaded_by(nl, nb, m))
                for blk in range(BLK):
                    dve.bn_stats(stats[:, blk, :], xt[:, m, blk, :]).then_inc(ln_stats.handle, 1)
                wait(dve, ln_stats, nl, nb, 2)
                alone(dve, dve_passed)
                for blk in range(BLK):
                    dve.bn_aggr(mv[:, blk, :], stats[:, blk, :]).then_inc(ln_stats.handle, 1)

            def normalise(nl, nb, m):
                wait(dve, ln_rstd, nl, nb, 2)
                for blk in range(BLK):
                    last = dve.tensor_scalar(xn[:, blk, :], xt[:, m, blk, :], mv[:, blk, 0:1], rstd[:, blk:blk + 1],
                                             ALU.subtract, ALU.mult)
                last.then_inc(xn_done.handle, 1)

            ln_stats_of(0, 0, 0)
            normalise(0, 0, 0)
            dve.wait_ge(w0_hi, 2)
            dve.tensor_tensor(wB[:, 1, :], big[:, 0:N_QKV], wB[:, 0, :].bitcast(F32), ALU.subtract).then_inc(w0_lo, 1)
            dve.tensor_tensor(wA[:, 1, N_GU0:], big[:, N_QKV:N_QKV + N_WO], wA[:, 0, N_GU0:].bitcast(F32),
                              ALU.subtract).then_inc(w0_lo, 1)
            dve.wait_ge(const_hi, 1)
            for c, (w, at, n) in enumerate(LUT_PIECES):
                idx, term, total = idx_slot(c, n), flat(prob, n), flat(pvT, n)
                dve.wait_ge(idx_loaded[c % 2], 16 * (c // 2 + 1))
                dve.wait_ge(w0_lo, 2 + c)
                for k in range(LUT):
                    dve.tensor_scalar(total if k == 0 else term, idx, float(k), lut[:, k:k + 1], ALU.is_equal,
                                      ALU.mult).then_inc(lut_step, 1)
                    dve.wait_ge(lut_step, 2 * LUT * c + 2 * k + 1)
                    if k == 0:
                        dve.memset(term[:, 0:1], 0.0).then_inc(lut_step, 1)
                    else:
                        dve.tensor_tensor(total, total, term, ALU.add).then_inc(lut_step, 1)
                    dve.wait_ge(lut_step, 2 * LUT * c + 2 * k + 2)
                dve.wait_ge(w0_hi, 3 + c)
                dve.tensor_tensor(store(w)[:, 1, at:at + n], total, store(w)[:, 0, at:at + n].bitcast(F32),
                                  ALU.subtract).then_inc(w0_lo, 1)
            dve.sem_inc(raw_lo, 2)

            def late(c0, c1):
                for c in range(c0, c1):
                    w, at, _ = LATE[c]
                    dve.wait_ge(late_hi, c + 1)
                    dve.tensor_tensor(store(w)[:, 1, at:at + LATE_CHUNK], late_slot(c),
                                      store(w)[:, 0, at:at + LATE_CHUNK].bitcast(F32), ALU.subtract).then_inc(late_lo, 1)

            def step(rnd, s, kind, j, batch):
                layer, b, n = batch
                if kind == "QK" and layer == 0:
                    wait(dve, qk_hi, layer, b, 1)
                    dve.tensor_tensor(split[:, 0:4:3, :, :].rearrange("p a b c -> p a (b c)").bitcast(F32R),
                                      banks(rnd, s)[:, :, :],
                                      split[:, 1:3, :, :].rearrange("p a b c -> p a (b c)"), ALU.subtract)\
                        .then_inc(read_out(rnd, s), 1)
                elif kind == "QK":
                    unit_filled(dve, rnd, s)
                    dve.tensor_tensor(ropet[:, :, :], banks(rnd, s)[:, :, :].rearrange("p a (t s) -> p (a t) s", t=2),
                                      rope[:, 0:1, :].broadcast_to([P, 4, S]), ALU.mult).then_inc(read_out(rnd, s), 1)
                elif kind == "ROT":
                    unit_filled(dve, rnd, s)
                    for qk in range(2):
                        last = dve.tensor_tensor(split[:, 3 * qk, :, :],
                                                 banks(rnd, s)[:, qk, :].rearrange("p (t s) -> p t s", t=2),
                                                 rope[:, 1:2, :].broadcast_to([P, 2, S]), ALU.mult)
                    last.then_inc(read_out(rnd, s), 1)
                elif kind == "ROTLO":
                    wait(dve, qk_hi, layer, b, 1)
                    dve.tensor_tensor(split[:, 0:4:3, :, :].rearrange("p a b c -> p a (b c)").bitcast(F32R),
                                      ropet.rearrange("p (a t) s -> p a (t s)", t=2),
                                      split[:, 1:3, :, :].rearrange("p a b c -> p a (b c)"), ALU.subtract)\
                        .then_inc(qk_lo.handle, 1)
                    wait(dve, qk_lo, layer, b, 1)
                elif kind == "LNS":
                    ln_stats_of(layer, b, n)
                elif kind == "LNN":
                    normalise(layer, b, n)
                elif kind == "X":
                    wait(dve, x_hi, layer, b, 1)
                    dve.tensor_tensor(xT[:, 1, :, :].rearrange("p a b -> p (a b)"), banks(rnd, s)[:, 0, :],
                                      xT[:, 0, :, :].rearrange("p a b -> p (a b)").bitcast(F32), ALU.subtract)\
                        .then_inc(read_out(rnd, s), 1)
                elif kind == "RAW":
                    if last_of_layer0(layer, b):
                        late(0, N_LATE_B)
                elif kind == "LATE":
                    dve.wait_ge(raw_hi, b + 1)
                    dve.tensor_tensor(wD[:, 1, bass.ds(b * STREAM_CHUNK, STREAM_CHUNK)],
                                      big[:, n * SLOT:n * SLOT + STREAM_CHUNK],
                                      wD[:, 0, bass.ds(b * STREAM_CHUNK, STREAM_CHUNK)].bitcast(F32),
                                      ALU.subtract).then_inc(raw_lo, 1)
                    if last_of_layer0(layer, b):
                        late(N_LATE_B, len(LATE) - 1)
                elif kind == "LT":
                    unit_filled(dve, rnd, s)
                    dve.tensor_copy(lg[:, :, :], banks(rnd, s)[:, 0, 0:BLK * NE].rearrange("p (k e) -> p k e", k=BLK))\
                        .then_inc(read_out(rnd, s), 1)
                    unit_read(dve, rnd, s)
                    alone(dve, dve_passed)
                    for blk in range(BLK):
                        dve.max(m8[:, blk, :], lg[:, blk, :]).then_inc(top_step.handle, 1)
                    wait(dve, top_step, layer, b, 2)
                    alone(dve, dve_passed)
                    for blk in range(BLK):
                        dve.max_index(i8[:, blk, :], m8[:, blk, :], lg[:, blk, :]).then_inc(top_step.handle, 1)
                    dve.tensor_scalar(nmax[:, :], m8[:, :, 0], -1.0, None, ALU.mult).then_inc(top_step.handle, 1)
                    wait(dve, top_step, layer, b, 4)
                    dve.tensor_copy(i8f[:, :, :], i8[:, :, :]).then_inc(top_step.handle, 1)
                    wait(dve, top_step, layer, b, 6)
                    for blk in range(BLK):
                        dve.tensor_scalar(sel0[:, blk, :], iota[:, :], i8f[:, blk, 0:1], None, ALU.is_equal)\
                            .then_inc(top_step.handle, 1)
                    wait(dve, top_step, layer, b, 8)
                    for blk in range(BLK):
                        dve.scalar_tensor_tensor(sel1[:, blk, :], iota[:, :], i8f[:, blk, 1:2], sel0[:, blk, :],
                                                 ALU.is_equal, ALU.add).then_inc(top_step.handle, 1)
                    wait(dve, exps_done, layer, b, 2)
                    dve.reciprocal(rsum[:, :], esum[:, :]).then_inc(top_step.handle, 1)
                    wait(dve, top_step, layer, b, 11)
                    for blk in range(BLK):
                        for at in (0, 32):
                            dve.scalar_tensor_tensor(comb[:, blk, at:at + NE], ex[:, blk, :], rsum[:, blk:blk + 1],
                                                     sel1[:, blk, :], ALU.mult, ALU.mult).then_inc(comb_done.handle, 1)
                elif kind == "CT":
                    wait(dve, comb_hi, layer, b, 1)
                    dve.tensor_tensor(combT[32:40, :], banks(rnd, s)[32:40, 0, 0:S], combT[32:40, :].bitcast(F32),
                                      ALU.subtract).then_inc(read_out(rnd, s), 1)
                elif kind == "MAX":
                    unit_filled(dve, rnd, s)
                    heads = slice(j, H, NPAIR)
                    dve.tensor_reduce(mx[:, 0, heads], banks(rnd, s)[:, :, 0:P], AX.X, ALU.max)
                    dve.tensor_reduce(mx[:, 1, heads], banks(rnd, s)[:, :, S:2 * S], AX.X, ALU.max)\
                        .then_inc(read_out(rnd, s), 1)
                elif kind == "PV":
                    wait(dve, pv_done, layer, b, j + 1)
                    dve.tensor_copy(pvT[:, j, :], pv[:, 0, :]).then_inc(pv_out.handle, 1)
                elif kind == "TR":
                    unit_filled(dve, rnd, s)
                    heads = banks(rnd, s)[:, :, :].rearrange("p k (h d) -> p k h d", d=2 * HD)
                    dve.reciprocal(rden[:, :, :], heads[:, :, :, HD]).then_inc(den_done.handle, 1)
                    wait(dve, den_done, layer, b, 1)
                    dve.tensor_tensor(o_tok.rearrange("p k (h d) -> p k h d", h=H), heads[:, :, :, 0:HD],
                                      rden[:, :, :].unsqueeze(3).broadcast_to([P, BLK, H, HD]), ALU.mult)\
                        .then_inc(read_out(rnd, s), 1)
                elif kind == "OT":
                    wait(dve, o_hi, layer, b, 1)
                    dve.tensor_tensor(oT[:, 1, :, :].rearrange("p a b -> p (a b)"), banks(rnd, s)[:, 0, :],
                                      oT[:, 0, :, :].rearrange("p a b -> p (a b)").bitcast(F32), ALU.subtract)\
                        .then_inc(read_out(rnd, s), 1)
                elif kind == "PROJ":
                    wait(dve, acc_ready, layer, b, 1)
                    dve.tensor_tensor(xt[:, n, :, :], acc[:, :, :], xt[:, n, :, :], ALU.add).then_inc(y_done.handle, 1)
                    if last_of_layer0(layer, b):
                        late(len(LATE) - 1, len(LATE))
                elif kind == "G":
                    wait(dve, tanh_done, layer, b, j + 1)
                    dve.scalar_tensor_tensor(ga[:, j % 2, :], th[:, j % 2, :], 1.0, gu[j % 2][:, 0, :], ALU.add, ALU.mult)\
                        .then_inc(gate_done.handle, 1)
                    wait(dve, gate_done, layer, b, j + 1)
                    dve.scalar_tensor_tensor(hb[:, j % 2, :], ga[:, j % 2, :], 0.5, gu[j % 2][:, 1, :], ALU.mult,
                                             ALU.mult).then_inc(hid_done.handle, 1)
                elif kind == "H":
                    wait(dve, h_hi, layer, b, j + 1)
                    dve.tensor_tensor(hs[:, j % 2, 1, :], hb[:, j % 2, :], hs[:, j % 2, 0, :].bitcast(F32),
                                      ALU.subtract).then_inc(h_lo.handle, 1)

            walk(dve, step)

        @block.gpsimd
        def _(pool):
            prime(pool, "POOL")
            pool.wait_ge(const_set, N_CONST_SET)

            def rstd_of(nl, nb):
                wait(pool, ln_stats, nl, nb, 4)
                alone(pool, pool_passed)
                pool.tensor_scalar(vareps[:, :], mv[:, :, 1], EPS, None, ALU.add).then_inc(ln_rstd.handle, 1)
                wait(pool, ln_rstd, nl, nb, 1)
                pool.tensor_tensor(rstd[:, :], vareps[:, :], negh[:, :], ALU.pow).then_inc(ln_rstd.handle, 1)

            rstd_of(0, 0)

            def step(rnd, s, kind, j, batch):
                layer, b, n = batch
                if kind == "ROT":
                    unit_read(pool, rnd, s)
                    for qk in range(2):
                        last = pool.tensor_tensor(ropet[:, 2 * qk:2 * qk + 2, :], ropet[:, 2 * qk:2 * qk + 2, :],
                                                  split[:, 3 * qk, :, :], ALU.add)
                    last.then_inc(rope_sum.handle, 1)
                elif kind == "LNS":
                    rstd_of(layer, b)
                elif kind == "ST":
                    unit_read(pool, rnd, s)
                    alone(pool, pool_passed)
                    diag = prob_of(rnd[0], j)[:, 0:2].rearrange("p a r c -> p (a r) c")
                    pool.affine_select(out=diag, in_=diag, compare_op=ALU.is_ge, fill=0.0, base=0,
                                       pattern=[[0, 4], [1, P]], channel_multiplier=-1)\
                        .then_inc(masked.handle, 1)
                elif kind == "G" and layer == 1 and j >= TS:
                    wait(pool, hid_done, layer, b, j + 1)
                    if (j - TS) % 4 == 0:
                        unit_read(pool, rnd, f"CB{(j - TS) // 4}")
                    pool.tensor_tensor(hb[:, j % 2, :], hb[:, j % 2, :], combB[:, j - TS, :], ALU.mult)\
                        .then_inc(weighted.handle, 1)

            walk(pool, step)


def layout(a):
    f = np.float32
    order = np.array([(4 * jj + 2 * t + r) * HD + d for t in range(2) for jj in range(4) for r in range(2)
                      for d in range(HD)])
    rot = np.array([(o // HD) * HD + (o % HD + HD // 2) % HD for o in order])

    def rows(w):
        return np.ascontiguousarray(w.reshape(-1, P, w.shape[1]).transpose(1, 0, 2)).reshape(P, -1)

    def padded(w, n, fill=0):
        out = np.full((n,) + w.shape[1:], fill, w.dtype)
        out[:w.shape[0]] = w
        return out

    def gate_up(g, u):
        w = np.stack([g.reshape(-1, P, KT, P), u.reshape(-1, P, KT, P)])
        return np.ascontiguousarray(w.transpose(4, 1, 3, 0, 2)).reshape(P, -1)

    wqkv = a["L0_attn_W_qkv"]
    qkv0 = np.concatenate([wqkv[0:D][order], wqkv[D:2 * D][order], wqkv[2 * D:]]).T
    w0_lin = np.concatenate([rows(qkv0), rows(a["L0_attn_W_proj"].T)], axis=1)
    gi, ui, di = a["L0_ffn_gate_idx"], a["L0_ffn_up_idx"], a["L0_ffn_down_idx"]
    idx0 = np.concatenate([gate_up(padded(gi, T0 * P, LUT), padded(ui, T0 * P, LUT)),
                           rows(padded(np.ascontiguousarray(di.T), T0 * P, LUT))], axis=1)
    wq, wk, wv = a["L1_attn_Wq"], a["L1_attn_Wk"], a["L1_attn_Wv"]
    g1 = np.concatenate([padded(a["L1_ffn_sw1"], TS * P), a["L1_ffn_w1"].reshape(NE * EI, D)])
    u1 = np.concatenate([padded(a["L1_ffn_sw2"], TS * P), a["L1_ffn_w2"].reshape(NE * EI, D)])
    w1_stream = np.concatenate([rows(np.concatenate([wq[order], wk[order], wv]).T),
                                rows(padded(a["L1_ffn_gate_w"], P).T), gate_up(g1, u1)], axis=1)
    dn1 = np.concatenate([padded(np.ascontiguousarray(a["L1_ffn_sw3"].T), TS * P),
                          a["L1_ffn_w3"].transpose(0, 2, 1).reshape(NE * EI, D)])
    w1_late = np.concatenate([rows(dn1), rows(np.concatenate([wq[rot], wk[rot]]).T), rows(a["L1_attn_Wo"].T)], axis=1)

    inv_freq = 1.0 / 10000.0 ** (np.arange(0, HD, 2, dtype=f) / HD)
    freqs = np.einsum("i,j->ij", np.arange(S, dtype=f), inv_freq)
    emb = np.concatenate((freqs, freqs), axis=-1)
    d = np.arange(P) % HD
    sign = np.where(d < HD // 2, -1.0, 1.0).astype(f)[:, None]
    rope = np.stack([np.cos(emb).astype(f).T[d], np.sin(emb).astype(f).T[d] * sign], axis=1)
    q, k = np.arange(P)[:, None], np.arange(P)[None, :]
    mask = np.where(k > q, -1e30, 0.0).astype(f)
    owner = (np.arange(TE * P) // EI)[None, :]
    e = np.arange(64)[:, None]
    esel = (((e < NE) & (e == owner)) | ((e >= 32) & (e - 32 == owner))).astype(f)
    return {
        "x_in": a["L0_attn_x"], "w0_lin": w0_lin, "idx0": idx0, "lut_in": a["L0_ffn_lut"], "w1_stream": w1_stream,
        "w1_late": w1_late, "rope_in": rope.astype(f), "ident_in": np.eye(P, dtype=f),
        "mask_in": np.stack([mask, mask], axis=1).reshape(P, 2 * P), "esel_in": esel,
        "iota_in": np.tile(np.arange(NE, dtype=f), (P, 1)),
    }


def kernel(**inputs):
    import concourse.bacc as bacc
    from concourse.bass_utils import run_bass_kernel_spmd

    arrays = {n: np.ascontiguousarray(v) for n, v in layout({k: np.asarray(v) for k, v in inputs.items()}).items()}
    nc = bacc.Bacc("TRN2", target_bir_lowering=False, num_devices=1)
    args = {n: nc.dram_tensor(n, v.shape, mybir.dt.from_np(v.dtype), kind="ExternalInput").ap()
            for n, v in arrays.items()}
    y = nc.dram_tensor("y_out", (B, S, D), F32, kind="ExternalOutput").ap()
    build(nc, y_out=y, **args)
    r = run_bass_kernel_spmd(nc, [arrays], core_ids=[0])
    return r.results[0]["y_out"]
```

```python
from contextlib import ExitStack

import numpy as np

import concourse.bass as bass
from concourse import mybir

F32 = mybir.dt.float32
F32R = mybir.dt.float32r
BF16 = mybir.dt.bfloat16
I32 = mybir.dt.int32
U32 = mybir.dt.uint32
ALU = mybir.AluOpType
ACT = mybir.ActivationFunctionType
AX = mybir.AxisListType

P = 128
B = 16
S = 256
D = 256
KT = D // P
BLK = S // P
H = 16
HD = D // H
NPAIR = H // 2
LUT = 16
INTER = 688
NE = 8
EI = 176
SI = 352
T0 = -(-INTER // P)
TS = -(-SI // P)
TE = NE * EI // P
NF = (T0, TS + TE)
SCALE = (1.0 / 16.0, 1.0 / 4.0)
EPS = 1e-5

GU_TILE = KT * 2 * P
N_GU0, N_DN0 = T0 * GU_TILE, T0 * D
N_GU1, N_DN1 = NF[1] * GU_TILE, NF[1] * D
N_QKV, N_WO, N_ROT, N_RT = KT * 3 * D, KT * D, KT * 2 * D, KT * P
N_STREAM = N_QKV + N_RT + N_GU1
STREAM_CHUNK = N_STREAM // B
LATE_CHUNK = 512
SLOT = STREAM_CHUNK
N_SLOTS = 5

CHUNK = 512
N_CHUNKS = (N_GU0 + N_DN0) // CHUNK
PE_CHUNKS, DVE_CHUNKS, POOL_CHUNK = range(0, 5), range(5, 8), 8
assert len(PE_CHUNKS) + len(DVE_CHUNKS) + 1 == N_CHUNKS and N_GU0 % CHUNK == 0 == N_DN0 % CHUNK
IDX_LOADS = ((0, 2), (5, 6), (8, 9), (2, 5), (6, 8))
MASKS = 8
LATE = [("B", c, N_DN1 + c) for c in range(0, N_QKV, LATE_CHUNK)] \
    + [("A", c, c) for c in range(0, N_GU0, LATE_CHUNK)] + [("A", N_GU0, N_GU0)]
N_LATE_B = N_QKV // LATE_CHUNK
LATE_SLOTS = 3
CAST_ORDER = (0, 5, 1, 2, 6, 3, 4, 7)
HI_ORDER = (("pe", 0), ("dve", 0), ("pe", 1), ("pe", 2), ("dve", 1), ("pe", 3), ("pool", 0), ("pe", 4), ("dve", 2))
LO_AFTER = {10: (0,), 18: (1,), 20: (2,), 29: (3,), 34: (4,), 39: (5, 6)}
N_CONST, N_CONST_SET = 4, 5


def late_for_dn(f):
    return N_LATE_B + (f * D) // LATE_CHUNK + 1


PREV = ("NM", "ST", "PV", "TR", "OT", "PROJ", "DP")
NEXT = ("LNS", "LNN")


def steps_of(kind):
    return lambda *js: [(kind, j) for j in js]


ST, STK, PV, MAX, G, H_, D_, DP = (steps_of(kind) for kind in ("ST", "STK", "PV", "MAX", "G", "H", "D", "DP"))


HELD = 3
STEPS = (
    DP(0) + ["X"] + DP(1, 2) + ["NM", "QK"] + G(0) + ST(0, 1) + STK(0) + ST(2, 3) + STK(1) + G(1) + H_(0)
    + PV(0) + ST(4, 5) + STK(2) + PV(1) + ST(6, 7) + H_(1) + STK(3) + PV(2) + G(2) + MAX(0) + PV(3)
    + ["V", "TR"] + H_(2) + G(3) + ["OT"] + MAX(1, 2) + ["PROJ"] + MAX(3) + D_(0) + H_(3) + MAX(4) + ["RAW"]
    + G(4) + D_(1) + ["LNS"] + MAX(5) + H_(4) + G(5) + MAX(6) + D_(2) + ["LNN"] + MAX(7) + H_(5) + ["LATE"],
    DP(0) + ["X", "NM"] + DP(1, 2) + ["QK", "ROT"] + ST(0, 1) + G(0) + ["ROTHI", "ROTLO"] + STK(0) + ST(2, 3)
    + STK(1) + H_(0) + PV(0) + ST(4) + G(1) + ST(5) + STK(2) + H_(1) + PV(1) + G(2) + ST(6, 7) + STK(3) + PV(2)
    + MAX(0) + PV(3) + ["VR", "TR"] + MAX(1) + ["OT"] + MAX(2) + ["LT", "PROJ"] + MAX(3) + D_(0) + H_(2)
    + ["CT"] + MAX(4) + ["CB0"] + G(3) + D_(1) + ["CB1"] + G(4) + H_(3) + MAX(5) + G(5) + ["CB2"] + H_(4)
    + D_(2) + ["LNS"] + MAX(6) + G(6) + H_(5) + D_(3) + G(7) + H_(6) + D_(4) + ["LNN"] + MAX(7) + G(8) + H_(7)
    + D_(5) + G(9) + H_(8) + D_(6) + G(10) + H_(9) + D_(7) + G(11) + H_(10) + D_(8) + G(12) + H_(11) + D_(9)
    + G(13) + H_(12) + D_(10) + H_(13),
)
UNIT_KINDS = ("X", "NM", "QK", "ROT", "TR", "V", "VR", "OT", "LT", "CT", "CB0", "CB1", "CB2", "MAX")
UNITS = [[u for u in steps if (u[0] if isinstance(u, tuple) else u) in UNIT_KINDS or (u[0] == "ST" and u[1] < NPAIR)]
         for steps in STEPS]
assert all(len(u) % 2 == 0 for u in UNITS)

CREDIT = 3


class Counter:

    def __init__(self, handle, per, by=1):
        self.handle, self.per, self.by = handle, per, by

    def at(self, layer, b, k):
        if layer == 0:
            return b * (self.per[0] * self.by) + (CREDIT + k) * self.by
        return b * (self.per[1] * self.by) + (CREDIT + B * self.per[0] + k) * self.by


def build(nc, x_in, w0_lin, idx0, lut_in, w1_stream, w1_late, rope_in, ident_in, mask_in, esel_in, iota_in, y_out):
    x1 = nc.dram_tensor("x1_scratch", (B, BLK, P, D), F32, kind="Internal").ap()
    esel_copy = nc.dram_tensor("esel_copy", (64, TE * P), F32, kind="Internal").ap()
    src = (x_in.rearrange("b (k p) d -> b p k d", p=P), x1.rearrange("b k p d -> b p k d"))
    dst = (x1.rearrange("b k p d -> b p k d"), y_out.rearrange("b (k p) d -> b p k d", p=P))

    with ExitStack() as ctx:
        def sb(name, shape, dt=F32):
            return ctx.enter_context(nc.sbuf_tensor(name, shape, dt))

        counters = []

        def counter(name, per, by=1):
            c = Counter(ctx.enter_context(nc.semaphore(name)), per, by)
            counters.append(c)
            return c

        def sem(name):
            return ctx.enter_context(nc.semaphore(name))

        wA = sb("wA", [P, 2, N_DN1], F32R)
        wB = sb("wB", [P, 2, N_QKV], F32R)
        with nc.sbuf_tensor("wD", [P, 2, N_STREAM], F32R) as wD:
            pass
        idx = sb("idx", [P, N_CHUNKS * CHUNK], I32)
        idxb = sb("idxb", [P, POOL_CHUNK * CHUNK], BF16)
        lutp = sb("lutp", [P, 3, LUT])
        lutr = sb("lutr", [P, 2, LUT])
        lutb = sb("lutb", [P, LUT], BF16)
        diag_lut = sb("diag_lut", [P, LUT * 3, P], BF16)
        masks = sb("masks", [P, MASKS, CHUNK], BF16)
        own_mask = sb("own_mask", [P, 2, CHUNK], BF16)
        own_sum = sb("own_sum", [P, 2, CHUNK])
        pool_term = sb("pool_term", [P, CHUNK])
        pool_sum = sb("pool_sum", [P, CHUNK])
        used = 4 * N_CHUNKS * CHUNK + 2 * POOL_CHUNK * CHUNK + 22 * LUT + 6 * LUT * P + 2 * MASKS * CHUNK + 4 * CHUNK \
            + 8 * CHUNK + 8 * CHUNK
        sb("rest_of_wD", [P, (2 * N_STREAM * 4 - used) // 4])
        assert N_GU0 + N_WO == N_DN1 and N_ROT + N_WO == N_QKV
        GU = (wA[:, :, 0:N_GU0].rearrange("p s (f k g c) -> p s f k g c", f=T0, k=KT, g=2),
              wD[:, :, N_QKV + N_RT:].rearrange("p s (f k g c) -> p s f k g c", f=NF[1], k=KT, g=2))
        QKV = (wB[:, :, :].rearrange("p s (k c) -> p s k c", k=KT), wD[:, :, 0:N_QKV].rearrange("p s (k c) -> p s k c", k=KT))
        WO = (wA[:, :, N_GU0:].rearrange("p s (k c) -> p s k c", k=KT), wB[:, :, N_ROT:].rearrange("p s (k c) -> p s k c", k=KT))
        ROTW = wB[:, :, 0:N_ROT].rearrange("p s (k c) -> p s k c", k=KT)
        RTW = wD[:, :, N_QKV:N_QKV + N_RT].rearrange("p s (k c) -> p s k c", k=KT)

        ident = sb("ident", [P, P])
        identb = sb("identb", [P, P], BF16)
        maskb = sb("maskb", [P, 2, P], BF16)
        rope = sb("rope", [P, 2, S])
        iota = sb("iota", [P, NE])
        lut = sb("lut", [P, LUT])
        negh = sb("negh", [P, BLK])

        xt = sb("xt", [P, 2, BLK, D])
        yt = sb("yt", [P, BLK, D])
        stats = sb("stats", [P, BLK, 6])
        mv = sb("mv", [P, BLK, 2])
        vareps = sb("vareps", [P, BLK])
        rstd = sb("rstd", [P, BLK])
        xn = sb("xn", [P, BLK, D])
        xT = sb("xT", [P, 2, KT, S], F32R)
        split = sb("split", [P, 4, 2, S])
        stk = sb("stk", [P, 2, NPAIR, S], F32R)
        stkf = stk[:, :, :, :].bitcast(F32)
        vaug = sb("vaug", [P, BLK, H, 2 * HD])
        mx = sb("mx", [P, BLK, H])
        nmT = sb("nmT", [H, S])
        prob = sb("prob", [P, 2, 3, 2, P])
        pvT = sb("pvT", [P, 4, S])
        rden = sb("rden", [P, BLK, H])
        o_tok = pvT[:, 0:2, :]
        oT = sb("oT", [P, 2, KT, S], F32R)
        th = sb("th", [P, 2, S])
        ga = sb("ga", [P, 2, S])
        hb = sb("hb", [P, 2, S])
        hs = sb("hs", [P, 3, 2, S], F32R)
        big = sb("big", [P, N_SLOTS * SLOT + 16])
        combB = big[:, 0:TE * S].rearrange("p (t s) -> p t s", t=TE)
        ropet = pvT[:, :, :]
        lgT = nmT[0:NE, :]
        lg = sb("lg", [P, BLK, NE])
        m8 = sb("m8", [P, BLK, 8])
        i8 = sb("i8", [P, BLK, 8], U32)
        i8f = sb("i8f", [P, BLK, 8])
        nmax = sb("nmax", [P, BLK])
        ex = sb("ex", [P, BLK, NE])
        esum = sb("esum", [P, BLK])
        rsum = sb("rsum", [P, BLK])
        sel0 = sb("sel0", [P, BLK, NE])
        sel1 = sb("sel1", [P, BLK, NE])
        comb = sb("comb", [P, BLK, 40])
        combT = sb("combT", [40, S], F32R)

        with nc.sbuf_tensor("wC", [P, 2, N_DN0], F32R) as wC:
            pass
        probx = sb("probx", [P, 12 * P])
        esel = sb("esel", [64, TE, P], F32R)
        assert 12 * P + TE * P <= 2 * N_DN0
        DN = (wC[:, :, :].rearrange("p s (f c) -> p s f c", f=T0), wA[:, :, :].rearrange("p s (f c) -> p s f c", f=NF[1]))

        pair = [ctx.enter_context(nc.psum_tensor(f"pair{n}", [P, 2, 512], F32)) for n in "ab"]
        pv = ctx.enter_context(nc.psum_tensor("pv", [P, 2, S], F32))
        acc = ctx.enter_context(nc.psum_tensor("acc", [P, BLK, D], F32))
        gu = [ctx.enter_context(nc.psum_tensor(f"gu{n}", [P, 2, S], F32)) for n in range(2)]

        unit_ready = counter("unit_ready", (len(UNITS[0]), len(UNITS[1])))
        pair_done = [counter(f"pair_done_{n}", (len(UNITS[0]) // 2, len(UNITS[1]) // 2)) for n in "ab"]
        ln_stats = counter("ln_stats", (4, 4))
        ln_rstd = counter("ln_rstd", (2, 2))
        xn_done = counter("xn_done", (1, 1))
        x_hi = counter("x_hi", (1, 1))
        qk_hi = counter("qk_hi", (1, 1))
        qk_lo = counter("qk_lo", (0, 1))
        rope_sum = counter("rope_sum", (0, 1))
        stk_loaded = [counter(f"stk_loaded{n}", (6, 6), 16) for n in range(4)]
        nm_loaded = counter("nm_loaded", (2, 2), 16)
        masked = counter("masked", (8, 8))
        pv_done = counter("pv_done", (4, 4))
        pv_out = counter("pv_out", (4, 4))
        den_done = counter("den_done", (1, 1))
        o_hi = counter("o_hi", (1, 1))
        gu_ready = counter("gu_ready", NF)
        tanh_done = counter("tanh_done", NF)
        gate_done = counter("gate_done", NF)
        hid_done = counter("hid_done", NF)
        weighted = counter("weighted", (0, TE))
        h_hi = counter("h_hi", NF)
        h_lo = counter("h_lo", NF)
        dn_done = counter("dn_done", NF)
        acc_ready = counter("acc_ready", (1, 1))
        y_done = counter("y_done", (1, 1))
        y_stored = counter("y_stored", (1, 1), 16)
        top_step = counter("top_step", (0, 11))
        exps_done = counter("exps_done", (0, 2))
        comb_done = counter("comb_done", (0, 4))
        comb_hi = counter("comb_hi", (0, 1))
        MADE_BY = {
            "PE": (unit_ready, pv_done, gu_ready, dn_done, acc_ready),
            "ACT": (x_hi, qk_hi, o_hi, tanh_done, h_hi, exps_done, comb_hi),
            "DVE": (pair_done[0], pair_done[1], ln_stats, xn_done, qk_lo, pv_out, den_done, gate_done, hid_done,
                    h_lo, y_done, top_step, comb_done),
            "POOL": (ln_rstd, rope_sum, masked, weighted),
            "SP": (*stk_loaded, nm_loaded, y_stored),
        }
        assert sorted(id(c) for v in MADE_BY.values() for c in v) == sorted(id(c) for c in counters)
        x_loaded = [sem(f"x_loaded{n}") for n in range(2)]
        raw_loaded = [sem(f"raw_loaded{n}") for n in range(2)]
        raw_hi, raw_lo = sem("raw_hi"), sem("raw_lo")
        late_loaded = [sem(f"late_loaded{n}") for n in range(LATE_SLOTS)]
        late_hi, late_lo = sem("late_hi"), sem("late_lo")
        neg_half_set = sem("neg_half_set")
        table_loaded = sem("table_loaded")
        const_loaded, const_set = sem("const_loaded"), sem("const_set")
        esel_loaded = sem("esel_loaded")
        w0_loaded, w0_hi, w0_lo = sem("w0_loaded"), sem("w0_hi"), sem("w0_lo")
        idx_loaded = [sem(f"idx_loaded{n}") for n in range(len(IDX_LOADS))]
        lut_part, diag_ready, idx_cast = sem("lut_part"), sem("diag_ready"), sem("idx_cast")
        mask_ready, mask_used = sem("mask_ready"), sem("mask_used")
        own_step, pool_step = sem("own_step"), sem("pool_step")
        chunk_hi = [sem(f"chunk_hi_{n}") for n in ("pe", "dve", "pool")]
        pe_chunk_lo = sem("pe_chunk_lo")
        dve_passed, pool_passed, sp_passed = sem("dve_passed"), sem("pool_passed"), sem("sp_passed")

        def prime(eng, who):
            for c in MADE_BY[who]:
                eng.sem_inc(c.handle, CREDIT * c.by)

        def wait(eng, c, layer, b, k):
            eng.wait_ge(c.handle, c.at(layer, b, k))

        def alone(eng, passed):
            eng.sem_inc(passed, 1)

        def unit(layer, what):
            j = UNITS[layer].index(what)
            return j, j % 2, j // 2

        def unit_filled(eng, rnd, what):
            wait(eng, unit_ready, *rnd, unit(rnd[0], what)[0] + 1)

        def unit_read(eng, rnd, what):
            _, p, turn = unit(rnd[0], what)
            wait(eng, pair_done[p], *rnd, turn + 1)

        def banks_free(eng, rnd, what):
            _, p, turn = unit(rnd[0], what)
            wait(eng, pair_done[p], *rnd, turn)

        def banks(rnd, what):
            return pair[unit(rnd[0], what)[1]]

        def read_out(rnd, what):
            return pair_done[unit(rnd[0], what)[1]].handle

        def loaded_by(layer, b, n):
            return (b - n) * (16 // 2) + 16 * (1 + layer * (B // 2))

        def walk(eng, step, left_out=None):
            def go(rnd, prev, own, nxt):
                for s in STEPS[rnd[0]]:
                    kind, j = s if isinstance(s, tuple) else (s, None)
                    batch = prev if kind in PREV else nxt if kind in NEXT else own
                    if batch is not None:
                        step(rnd, s, kind, j, batch)
                    elif left_out is not None and s in UNITS[rnd[0]]:
                        left_out(rnd, s)

            for layer in range(2):
                go((layer, 0), (0, B - 1, 1) if layer else None, (layer, 0, 0), (layer, 1, 1))
                with eng.Fori(0, B // 2 - 1) as i:
                    for n in (1, 0):
                        b = i * 2 + (2 - n)
                        go((layer, b), (layer, b - 1, 1 - n), (layer, b, n), (layer, b + 1, 1 - n))
                go((layer, B - 1), (layer, B - 2, 0), (layer, B - 1, 1), None if layer else (1, 0, 0))
            go((1, B), (1, B - 1, 1), None, None)

        def last_of_layer0(layer, b):
            return layer == 0 and isinstance(b, int) and b == B - 1

        def prob_of(layer, u):
            if u % 4 < 2:
                return prob[:, u % 4]
            return (big[:, 2 * SLOT:2 * SLOT + 12 * P] if layer == 0 else probx[:, :])\
                .rearrange("p (u a r c) -> p u a r c", u=2, a=3, r=2)[:, u % 2]

        def dram_batch(view, b):
            return view[bass.ds(b, 1)].rearrange("a p k d -> (a p) k d")

        def flat(t, n, dt=None):
            dims = " ".join("abcde"[:len(t.shape) - 1])
            v = t[tuple(slice(None) for _ in t.shape)]
            v = v.rearrange(f"p {dims} -> p ({dims})") if len(t.shape) > 2 else v
            v = v[:, 0:n]
            return v.bitcast(dt) if dt is not None else v

        def store(w):
            return {"A": wA, "B": wB, "C": wC}[w]

        def late_slot(c):
            s = 2 + c % LATE_SLOTS
            return big[:, s * SLOT:s * SLOT + LATE_CHUNK]

        def chunk_of(c, part):
            at = c * CHUNK
            return wA[:, part, at:at + CHUNK] if at < N_GU0 else wC[:, part, at - N_GU0:at - N_GU0 + CHUNK]

        def index_load_of(c):
            return next(n for n, (c0, c1) in enumerate(IDX_LOADS) if c0 <= c < c1)

        block = ctx.enter_context(nc.Block())

        @block.sync
        def _(sp):
            prime(sp, "SP")
            def load_indices(n):
                c0, c1 = IDX_LOADS[n]
                sp.dma_start(idx[:, c0 * CHUNK:c1 * CHUNK], idx0[:, c0 * CHUNK:c1 * CHUNK]).then_inc(idx_loaded[n], 16)

            sp.dma_start(lut[:, :], lut_in.partition_broadcast(P)).then_inc(table_loaded, 16)
            load_indices(0)
            sp.dma_start(ident[:, :], ident_in).then_inc(table_loaded, 16)
            load_indices(1)
            load_indices(2)
            sp.dma_start(xt[:, 0, :, :], dram_batch(src[0], 0)).then_inc(x_loaded[0], 16)
            sp.dma_start(th[:, 0, :], mask_in).then_inc(const_loaded, 16)
            sp.dma_start(rope[:, :, :], rope_in).then_inc(const_loaded, 16)
            sp.dma_start(iota[:, :], iota_in).then_inc(const_loaded, 16)
            sp.dma_start(esel_copy, esel_in).then_inc(const_loaded, 16)
            load_indices(3)
            sp.dma_start(big[:, 0:N_QKV], w0_lin[:, 0:N_QKV]).then_inc(w0_loaded, 16)
            sp.dma_start(big[:, N_QKV:N_QKV + N_WO], w0_lin[:, N_QKV:]).then_inc(w0_loaded, 16)
            load_indices(4)
            sp.wait_ge(w0_lo, 2 + N_CHUNKS)

            def stack_rows(jj):
                for r in range(2):
                    p0 = 32 * jj + 16 * r
                    for c, parts in enumerate((slice(1, 3), slice(0, 3, 2), slice(1, 4, 2))):
                        q0 = 64 * r + 16 * c
                        sp.dma_start(stkf[q0:q0 + 16, :, 2 * jj:2 * jj + 2, :], split[p0:p0 + 16, parts, :, :])\
                            .then_inc(stk_loaded[jj].handle, 16)

            def load_x(layer, b, n):
                if layer == 1:
                    wait(sp, y_stored, layer, b, -2)
                    alone(sp, sp_passed)
                sp.dma_start(xt[:, n, :, :], dram_batch(src[layer], b)).then_inc(x_loaded[n], 16)

            def step(rnd, s, kind, j, batch):
                layer, b, n = batch
                if kind == "ROT" and isinstance(b, int) and b == 0:
                    sp.wait_ge(const_loaded, 16 * N_CONST)
                    wait(sp, dn_done, 0, B - 1, NF[0])
                    sp.dma_start(flat(esel, TE * P, F32), esel_copy).then_inc(esel_loaded, 16)
                elif kind == "NM":
                    unit_read(sp, rnd, s)
                    for r in range(2):
                        sp.dma_start(stkf[64 * r + 48:64 * r + 49, 0, :, :], nmT[8 * r:8 * r + 8, :])\
                            .then_inc(nm_loaded.handle, 16)
                elif kind == "STK":
                    if j == 0:
                        if layer == 0:
                            unit_read(sp, rnd, "QK")
                        else:
                            wait(sp, qk_lo, layer, b, 1)
                        alone(sp, sp_passed)
                    unit_filled(sp, rnd, ("ST", 2 * j + 1))
                    stack_rows(j)
                elif kind == "RAW":
                    sp.wait_ge(raw_lo, b + 1)
                    alone(sp, sp_passed)
                    sp.dma_start(big[:, n * SLOT:n * SLOT + STREAM_CHUNK],
                                 w1_stream[:, bass.ds(b * STREAM_CHUNK, STREAM_CHUNK)])\
                        .then_inc(raw_loaded[n], 16)
                    if last_of_layer0(layer, b):
                        wait(sp, pv_done, 0, b - 1, 4)
                        for c in range(LATE_SLOTS):
                            sp.dma_start(late_slot(c), w1_late[:, LATE[c][2]:LATE[c][2] + LATE_CHUNK])\
                                .then_inc(late_loaded[c % LATE_SLOTS], 16)
                elif kind == "LATE" and last_of_layer0(layer, b):
                    for c in range(LATE_SLOTS, len(LATE)):
                        sp.wait_ge(late_lo, c - LATE_SLOTS + 1)
                        sp.dma_start(late_slot(c), w1_late[:, LATE[c][2]:LATE[c][2] + LATE_CHUNK])\
                            .then_inc(late_loaded[c % LATE_SLOTS], 16)
                elif kind == "PROJ":
                    wait(sp, y_done, layer, b, 1)
                    alone(sp, sp_passed)
                    sp.dma_start(dram_batch(dst[layer], b), yt[:, :, :]).then_inc(y_stored.handle, 16)
                elif kind == "LNS":
                    load_x(layer, b, n)

            walk(sp, step)
            wait(sp, y_stored, 1, B - 1, 1)

        @block.tensor
        def _(pe):
            prime(pe, "PE")

            def three(out, lhs, rhs, start, stop=False, **more):
                pe.matmul(out, lhs(0), rhs(0), start=start, stop=False, **more)
                pe.matmul(out, lhs(0), rhs(1), start=False, stop=False, **more)
                return pe.matmul(out, lhs(1), rhs(0), start=False, stop=stop, **more)

            def left_out(rnd, s):
                wait(pe, unit_ready, *rnd, unit(rnd[0], s)[0])
                banks_free(pe, rnd, s)
                pe.sem_inc(unit_ready.handle, 1)
                pe.sem_inc(read_out(rnd, s), 1)

            for n in range(len(PE_CHUNKS)):
                if n >= 2:
                    pe.wait_ge(pe_chunk_lo, n - 1)
                for k in range(LUT):
                    pe.wait_ge(mask_ready, LUT * n + k + 1)
                    if n == 0:
                        pe.wait_ge(diag_ready, 3 * (k + 1))
                    for q in range(3):
                        mm = pe.matmul(pair[n % 2][:, 0, :], diag_lut[:, 3 * k + q, :], masks[:, k % MASKS, :],
                                       start=k == 0 and q == 0, stop=k == LUT - 1 and q == 2)
                    mm.then_inc(mask_used, 1)
            pe.wait_ge(const_set, N_CONST_SET)
            pe.wait_ge(w0_lo, 2 + N_CHUNKS)

            def step(rnd, s, kind, j, batch):
                layer, b, n = batch
                if kind in ("QK", "ROT"):
                    banks_free(pe, rnd, s)
                    if kind == "QK":
                        unit_read(pe, rnd, "X")
                        if layer == 1:
                            pe.wait_ge(raw_lo, 2 + B)
                    else:
                        pe.wait_ge(late_lo, N_LATE_B)
                    w = QKV[layer] if kind == "QK" else ROTW
                    for qk in range(2):
                        for t in range(2):
                            for kt in range(KT):
                                mm = three(banks(rnd, s)[:, qk, t * S:(t + 1) * S],
                                           lambda h: w[:, h, kt, (2 * qk + t) * P:(2 * qk + t + 1) * P],
                                           lambda h: xT[:, h, kt, :], start=kt == 0, stop=kt == KT - 1)
                    mm.then_inc(unit_ready.handle, 1)
                elif kind in ("V", "VR"):
                    banks_free(pe, rnd, s)
                    for blk in range(BLK):
                        for kt in range(KT):
                            mm = three(banks(rnd, s)[:, 0, blk * D:(blk + 1) * D],
                                       lambda h: xT[:, h, kt, blk * P:(blk + 1) * P],
                                       lambda h: QKV[layer][:, h, kt, 2 * D:3 * D], start=kt == 0, stop=kt == KT - 1)
                    if kind == "VR":
                        for kt in range(KT):
                            mm = three(banks(rnd, s)[:, 1, 0:S], lambda h: RTW[:, h, kt, :],
                                       lambda h: xT[:, h, kt, :], start=kt == 0, stop=kt == KT - 1)
                    mm.then_inc(unit_ready.handle, 1)
                elif kind == "LT":
                    banks_free(pe, rnd, s)
                    unit_read(pe, rnd, "VR")
                    for blk in range(BLK):
                        mm = pe.matmul(banks(rnd, s)[:, 0, blk * NE:(blk + 1) * NE], nmT[0:NE, blk * P:(blk + 1) * P],
                                       ident[0:NE, 0:NE], start=True, stop=True)
                    mm.then_inc(unit_ready.handle, 1)
                elif kind == "CT":
                    banks_free(pe, rnd, s)
                    wait(pe, comb_done, layer, b, 4)
                    for blk in range(BLK):
                        mm = pe.matmul(banks(rnd, s)[0:40, 0, blk * P:(blk + 1) * P], comb[:, blk, :], ident[:, :],
                                       start=True, stop=True)
                    mm.then_inc(unit_ready.handle, 1)
                elif kind in ("CB0", "CB1", "CB2"):
                    banks_free(pe, rnd, s)
                    if kind == "CB0":
                        pe.wait_ge(esel_loaded, 16)
                    unit_read(pe, rnd, "CT")
                    c = int(kind[2])
                    for x, t in enumerate(range(4 * c, min(4 * c + 4, TE))):
                        mm = pe.matmul(banks(rnd, s)[:, x // 2, (x % 2) * S:(x % 2 + 1) * S], esel[0:40, t, :],
                                       combT[:, :], start=True, stop=True)
                    mm.then_inc(unit_ready.handle, 1)
                elif kind == "MAX":
                    banks_free(pe, rnd, s)
                    if j % 2 == 0:
                        wait(pe, stk_loaded[j // 2], layer, b, 6)
                    for blk in range(BLK):
                        for r in range(2):
                            rows = slice(64 * r, 64 * r + 48)
                            pe.matmul(banks(rnd, s)[:, r, blk * S:(blk + 1) * S],
                                      stk[rows, 0, j, blk * P:(blk + 1) * P], stk[rows, 1, j, :],
                                      start=blk == 0, stop=False, skip_group_check=True)
                    for r in range(2):
                        diag = banks(rnd, s)[:, r, :].rearrange("p (a c) -> p a c", c=P)[:, 0:4:3, :]
                        mm = pe.matmul(diag, identb[:, :], maskb[:, :, :], start=False, stop=True,
                                       skip_group_check=True)
                    mm.then_inc(unit_ready.handle, 1)
                elif kind == "NM":
                    banks_free(pe, rnd, s)
                    unit_read(pe, (layer, b), ("MAX", NPAIR - 1))
                    for blk in range(BLK):
                        mm = pe.matmul(banks(rnd, s)[0:H, 0, blk * P:(blk + 1) * P], mx[:, blk, :], ident[:, :],
                                       start=True, stop=True)
                    mm.then_inc(unit_ready.handle, 1)
                elif kind == "ST":
                    banks_free(pe, rnd, s)
                    if j == 0:
                        wait(pe, nm_loaded, layer, b, 2)
                    for kb in (1, 0):
                        for r in range(2):
                            rows = slice(64 * r, 64 * r + 49)
                            mm = pe.matmul(banks(rnd, s)[:, r, (1 - kb) * S:(2 - kb) * S],
                                           stk[rows, 1, j, kb * P:(kb + 1) * P], stk[rows, 0, j, :],
                                           start=True, stop=True)
                    mm.then_inc(unit_ready.handle, 1)
                elif kind == "PV":
                    wait(pe, masked, layer, b, 2 * j + 2)
                    wait(pe, pv_out, layer, b, j)
                    for kb in range(BLK):
                        for x in range(4):
                            u, r, rows = 2 * j + x // 2, x % 2, slice(32 * x, 32 * x + 32)
                            if kb == 0:
                                pe.matmul(pv[rows, 0, :].rearrange("p (a c) -> p a c", a=2), vaug[:, 0, 4 * j + x, :],
                                          prob_of(rnd[0], u)[:, 1:3, r, :], start=True, stop=False,
                                          skip_group_check=True)
                            else:
                                mm = pe.matmul(pv[rows, 0, P:S], vaug[:, 1, 4 * j + x, :],
                                               prob_of(rnd[0], u)[:, 0, r, :], start=False, stop=True,
                                               skip_group_check=True)
                    mm.then_inc(pv_done.handle, 1)
                elif kind == "TR":
                    banks_free(pe, rnd, s)
                    wait(pe, pv_out, layer, b, 4)
                    for blk in range(BLK):
                        for g in range(4):
                            mm = pe.transpose(banks(rnd, s)[:, blk, g * P:(g + 1) * P],
                                              pvT[:, g, blk * P:(blk + 1) * P], ident[:, :])
                    mm.then_inc(unit_ready.handle, 1)
                elif kind == "OT":
                    banks_free(pe, rnd, s)
                    unit_read(pe, rnd, "TR")
                    for kt in range(KT):
                        for blk in range(BLK):
                            mm = pe.transpose(banks(rnd, s)[:, 0, kt * S + blk * P:kt * S + (blk + 1) * P],
                                              o_tok[:, blk, kt * P:(kt + 1) * P], ident[:, :])
                    mm.then_inc(unit_ready.handle, 1)
                elif kind == "X":
                    wait(pe, xn_done, layer, b, 1)
                    banks_free(pe, rnd, s)
                    for kt in range(KT):
                        for blk in range(BLK):
                            mm = pe.transpose(banks(rnd, s)[:, 0, kt * S + blk * P:kt * S + (blk + 1) * P],
                                              xn[:, blk, kt * P:(kt + 1) * P], ident[:, :])
                    mm.then_inc(unit_ready.handle, 1)
                elif kind == "PROJ":
                    unit_read(pe, rnd, "OT")
                    for blk in range(BLK):
                        for kt in range(KT):
                            mm = three(acc[:, blk, :], lambda h: oT[:, h, kt, blk * P:(blk + 1) * P],
                                       lambda h: WO[layer][:, h, kt, :], start=False, skip_group_check=True,
                                       stop=blk == BLK - 1 and kt == KT - 1)
                    mm.then_inc(acc_ready.handle, 1)
                elif kind == "G":
                    wait(pe, hid_done, layer, b, j - 1)
                    for g in range(2):
                        for kt in range(KT):
                            mm = three(gu[j % 2][:, g, :], lambda h: GU[layer][:, h, j, kt, g, :],
                                       lambda h: xT[:, h, kt, :], start=kt == 0, stop=kt == KT - 1)
                    mm.then_inc(gu_ready.handle, 1)
                elif kind in ("D", "DP"):
                    if kind == "DP":
                        j += NF[layer] - HELD
                    wait(pe, h_lo, layer, b, j + 1)
                    if j == 0:
                        wait(pe, y_done, layer, b, 0)
                    if layer == 1:
                        pe.wait_ge(late_lo, late_for_dn(j))
                    for blk in range(BLK):
                        mm = three(acc[:, blk, :], lambda h: hs[:, j % 3, h, blk * P:(blk + 1) * P],
                                   lambda h: DN[layer][:, h, j, :], start=j == 0 and blk == 0,
                                   skip_group_check=True)
                    mm.then_inc(dn_done.handle, 1)

            walk(pe, step, left_out)

        @block.scalar
        def _(act):
            prime(act, "ACT")
            for c in CAST_ORDER[:2]:
                act.wait_ge(idx_loaded[index_load_of(c)], 16)
                act.copy(idxb[:, c * CHUNK:(c + 1) * CHUNK], idx[:, c * CHUNK:(c + 1) * CHUNK]).then_inc(idx_cast, 1)
            act.wait_ge(table_loaded, 32)
            act.wait_ge(lut_part, 8)
            for k in range(LUT):
                for q in range(3):
                    act.activation(diag_lut[:, 3 * k + q, :], ident[:, :], ACT.Copy, scale=lutp[:, q, k:k + 1])\
                        .then_inc(diag_ready, 1)
            for c in CAST_ORDER[2:]:
                act.wait_ge(idx_loaded[index_load_of(c)], 16)
                act.copy(idxb[:, c * CHUNK:(c + 1) * CHUNK], idx[:, c * CHUNK:(c + 1) * CHUNK]).then_inc(idx_cast, 1)
            act.wait_ge(w0_loaded, 32)
            act.copy(wB[:, 0, :], big[:, 0:N_QKV]).then_inc(w0_hi, 1)
            act.copy(wA[:, 0, N_GU0:], big[:, N_QKV:N_QKV + N_WO]).then_inc(w0_hi, 1)
            for who, n in HI_ORDER:
                if who == "pe":
                    act.wait_ge(mask_used, LUT * (n + 1))
                    act.copy(chunk_of(PE_CHUNKS[n], 0), pair[n % 2][:, 0, :]).then_inc(chunk_hi[0], 1)
                elif who == "dve":
                    act.wait_ge(own_step, 1 + 2 * LUT * (n + 1))
                    act.copy(chunk_of(DVE_CHUNKS[n], 0), own_sum[:, n % 2, :]).then_inc(chunk_hi[1], 1)
                else:
                    act.wait_ge(pool_step, 2 * LUT - 1)
                    act.copy(chunk_of(POOL_CHUNK, 0), pool_sum[:, :]).then_inc(chunk_hi[2], 1)

            def late(c0, c1):
                for c in range(c0, c1):
                    w, at, _ = LATE[c]
                    act.wait_ge(late_loaded[c % LATE_SLOTS], 16 * (c // LATE_SLOTS + 1))
                    act.copy(store(w)[:, 0, at:at + LATE_CHUNK], late_slot(c)).then_inc(late_hi, 1)

            def step(rnd, s, kind, j, batch):
                layer, b, n = batch
                if kind == "QK" and layer == 0:
                    unit_filled(act, rnd, s)
                    act.copy(split[:, 1:3, :, :].rearrange("p a b c -> p a (b c)").bitcast(F32R),
                             banks(rnd, s)[:, :, :]).then_inc(qk_hi.handle, 1)
                elif kind == "ROTHI":
                    wait(act, rope_sum, layer, b, 1)
                    act.copy(split[:, 1:3, :, :].rearrange("p a b c -> p (a b c)").bitcast(F32R),
                             ropet.rearrange("p a s -> p (a s)")).then_inc(qk_hi.handle, 1)
                elif kind in ("V", "VR"):
                    unit_filled(act, rnd, s)
                    v = act.copy(vaug[:, :, :, 0:HD],
                                 banks(rnd, s)[:, 0, :].rearrange("p (k h d) -> p k h d", k=BLK, h=H))
                    if kind == "V":
                        v.then_inc(read_out(rnd, s), 1)
                    else:
                        act.copy(lgT, banks(rnd, s)[0:NE, 1, 0:S]).then_inc(read_out(rnd, s), 1)
                elif kind == "LT":
                    wait(act, top_step, layer, b, 5)
                    for blk in range(BLK):
                        act.activation(ex[:, blk, :], lg[:, blk, :], ACT.Exp, bias=nmax[:, blk:blk + 1],
                                       accum_out=esum[:, blk:blk + 1]).then_inc(exps_done.handle, 1)
                elif kind == "CT":
                    unit_filled(act, rnd, s)
                    act.copy(combT[:, :], banks(rnd, s)[0:40, 0, 0:S]).then_inc(comb_hi.handle, 1)
                elif kind in ("CB0", "CB1", "CB2"):
                    c = int(kind[2])
                    nt = min(4, TE - 4 * c)
                    unit_filled(act, rnd, s)
                    if c == 0:
                        wait(act, weighted, layer, b, 0)
                        act.wait_ge(late_lo, len(LATE))
                    act.copy(combB[:, 4 * c:4 * c + nt, :].rearrange("p a b -> p (a b)"),
                             banks(rnd, s)[:, :, :].rearrange("p a b -> p (a b)")[:, 0:nt * S])\
                        .then_inc(read_out(rnd, s), 1)
                elif kind == "NM":
                    unit_filled(act, rnd, s)
                    act.activation(nmT[:, :].bitcast(F32R), banks(rnd, s)[0:H, 0, 0:S], ACT.Copy, scale=-1.0)\
                        .then_inc(read_out(rnd, s), 1)
                elif kind == "RAW":
                    if last_of_layer0(layer, b):
                        late(0, N_LATE_B)
                elif kind == "ST":
                    unit_filled(act, rnd, s)
                    if j % 2 == 0:
                        wait(act, pv_done, layer, b, j // 2 - 1)
                    act.activation(prob_of(rnd[0], j).rearrange("p a r c -> p r a c"),
                                   banks(rnd, s)[:, :, P:2 * S].rearrange("p r (a c) -> p r a c", c=P), ACT.Exp,
                                   scale=SCALE[layer]).then_inc(read_out(rnd, s), 1)
                elif kind == "OT":
                    unit_filled(act, rnd, s)
                    act.copy(oT[:, 0, :, :].rearrange("p a b -> p (a b)"), banks(rnd, s)[:, 0, :])\
                        .then_inc(o_hi.handle, 1)
                elif kind == "X":
                    unit_filled(act, rnd, s)
                    act.copy(xT[:, 0, :, :].rearrange("p a b -> p (a b)"), banks(rnd, s)[:, 0, :]).then_inc(x_hi.handle, 1)
                elif kind == "LATE":
                    act.wait_ge(raw_loaded[n], (b - n) * 8 + 16)
                    act.copy(wD[:, 0, bass.ds(b * STREAM_CHUNK, STREAM_CHUNK)],
                             big[:, n * SLOT:n * SLOT + STREAM_CHUNK]).then_inc(raw_hi, 1)
                    if last_of_layer0(layer, b):
                        late(N_LATE_B, len(LATE) - 1)
                elif kind == "PROJ" and last_of_layer0(layer, b):
                    wait(act, acc_ready, layer, b, 1)
                    late(len(LATE) - 1, len(LATE))
                elif kind == "G":
                    wait(act, gu_ready, layer, b, j + 1)
                    wait(act, gate_done, layer, b, j - 1)
                    act.activation(th[:, j % 2, :], gu[j % 2][:, 0, :], ACT.Tanh, scale=0.5)\
                        .then_inc(tanh_done.handle, 1)
                elif kind == "H":
                    if layer == 1 and j >= TS:
                        wait(act, weighted, layer, b, j - TS + 1)
                    else:
                        wait(act, hid_done, layer, b, j + 1)
                    wait(act, dn_done, layer, b, j - 2)
                    act.copy(hs[:, j % 3, 0, :], hb[:, j % 2, :]).then_inc(h_hi.handle, 1)

            walk(act, step)

        @block.vector
        def _(dve):
            prime(dve, "DVE")
            dve.wait_ge(table_loaded, 32)
            dve.tensor_copy(identb[:, :], ident[:, :]).then_inc(const_set, 1)

            def ln_stats_of(nl, nb, m):
                dve.wait_ge(x_loaded[m], loaded_by(nl, nb, m))
                for blk in range(BLK):
                    dve.bn_stats(stats[:, blk, :], xt[:, m, blk, :]).then_inc(ln_stats.handle, 1)
                wait(dve, ln_stats, nl, nb, 2)
                alone(dve, dve_passed)
                for blk in range(BLK):
                    dve.bn_aggr(mv[:, blk, :], stats[:, blk, :]).then_inc(ln_stats.handle, 1)

            def normalise(nl, nb, m):
                wait(dve, ln_rstd, nl, nb, 2)
                for blk in range(BLK):
                    last = dve.tensor_scalar(xn[:, blk, :], xt[:, m, blk, :], mv[:, blk, 0:1], rstd[:, blk:blk + 1],
                                             ALU.subtract, ALU.mult)
                last.then_inc(xn_done.handle, 1)

            for q in range(3):
                left = lut[:, :] if q == 0 else lutr[:, q - 1, :]
                dve.tensor_copy(lutb[:, :], left).then_inc(lut_part, 1)
                dve.wait_ge(lut_part, 3 * q + 1)
                dve.tensor_copy(lutp[:, q, :], lutb[:, :]).then_inc(lut_part, 1)
                dve.wait_ge(lut_part, 3 * q + 2)
                if q < 2:
                    dve.tensor_tensor(lutr[:, q, :], left, lutp[:, q, :], ALU.subtract).then_inc(lut_part, 1)
                    dve.wait_ge(lut_part, 3 * q + 3)
            def own_mask_step(i):
                c = DVE_CHUNKS[i // LUT]
                dve.wait_ge(idx_cast, CAST_ORDER.index(c) + 1)
                dve.tensor_scalar(own_mask[:, i % 2, :], idxb[:, c * CHUNK:(c + 1) * CHUNK], float(i % LUT), None,
                                  ALU.is_equal).then_inc(own_step, 1)

            def own_sum_step(i):
                n, k = i // LUT, i % LUT
                total, mask = own_sum[:, n % 2, :], own_mask[:, i % 2, :]
                if k == 0:
                    dve.tensor_scalar(total, mask, lut[:, 0:1], None, ALU.mult).then_inc(own_step, 1)
                else:
                    dve.scalar_tensor_tensor(total, mask, lut[:, k:k + 1], total, ALU.mult, ALU.add).then_inc(own_step, 1)

            def pe_mask_step(m):
                c = PE_CHUNKS[m // LUT]
                dve.wait_ge(idx_cast, CAST_ORDER.index(c) + 1)
                if m >= MASKS:
                    dve.wait_ge(mask_used, m - MASKS + 1)
                dve.tensor_scalar(masks[:, m % MASKS, :], idxb[:, c * CHUNK:(c + 1) * CHUNK], float(m % LUT), None,
                                  ALU.is_equal).then_inc(mask_ready, 1)

            def chunk_lo(at, splits):
                who, n = HI_ORDER[at]
                c, hi, total = {"pe": (PE_CHUNKS, chunk_hi[0], pair[n % 2][:, 0, :]),
                                "dve": (DVE_CHUNKS, chunk_hi[1], own_sum[:, n % 2, :]),
                                "pool": ((POOL_CHUNK,), chunk_hi[2], pool_sum[:, :])}[who]
                dve.wait_ge(hi, n + 1)
                dve.tensor_tensor(chunk_of(c[n], 1), total, chunk_of(c[n], 0).bitcast(F32), ALU.subtract)\
                    .then_inc(w0_lo, 1)
                if who == "pe":
                    dve.wait_ge(w0_lo, splits)
                    dve.sem_inc(pe_chunk_lo, 1)

            n_own, n_masks = LUT * len(DVE_CHUNKS), LUT * len(PE_CHUNKS)
            own_mask_step(0)
            for m in range(MASKS):
                pe_mask_step(m)
            masks_made = MASKS
            ln_stats_of(0, 0, 0)
            for i in range(n_own):
                if i == 4:
                    normalise(0, 0, 0)
                dve.wait_ge(own_step, 2 * i + 1)
                if i + 1 < n_own:
                    own_mask_step(i + 1)
                else:
                    dve.sem_inc(own_step, 1)
                own_sum_step(i)
                while masks_made < min(n_masks, MASKS + (i + 1) * n_masks // n_own):
                    pe_mask_step(masks_made)
                    masks_made += 1
                for at in LO_AFTER.get(i, ()):
                    chunk_lo(at, at + 1)
            dve.wait_ge(w0_hi, 2)
            dve.tensor_tensor(wB[:, 1, :], big[:, 0:N_QKV], wB[:, 0, :].bitcast(F32), ALU.subtract).then_inc(w0_lo, 1)
            dve.tensor_tensor(wA[:, 1, N_GU0:], big[:, N_QKV:N_QKV + N_WO], wA[:, 0, N_GU0:].bitcast(F32),
                              ALU.subtract).then_inc(w0_lo, 1)
            for at in range(1 + max(LO_AFTER[max(LO_AFTER)]), N_CHUNKS):
                chunk_lo(at, 2 + at + 1)
            dve.wait_ge(const_loaded, 16 * N_CONST)
            dve.tensor_copy(maskb[:, :, :].rearrange("p a b -> p (a b)"), th[:, 0, :]).then_inc(const_set, 1)
            dve.sem_inc(raw_lo, 2)

            def late(c0, c1):
                for c in range(c0, c1):
                    w, at, _ = LATE[c]
                    dve.wait_ge(late_hi, c + 1)
                    dve.tensor_tensor(store(w)[:, 1, at:at + LATE_CHUNK], late_slot(c),
                                      store(w)[:, 0, at:at + LATE_CHUNK].bitcast(F32), ALU.subtract).then_inc(late_lo, 1)

            def step(rnd, s, kind, j, batch):
                layer, b, n = batch
                if kind == "QK" and layer == 0:
                    wait(dve, qk_hi, layer, b, 1)
                    dve.tensor_tensor(split[:, 0:4:3, :, :].rearrange("p a b c -> p a (b c)").bitcast(F32R),
                                      banks(rnd, s)[:, :, :],
                                      split[:, 1:3, :, :].rearrange("p a b c -> p a (b c)"), ALU.subtract)\
                        .then_inc(read_out(rnd, s), 1)
                elif kind == "QK":
                    unit_filled(dve, rnd, s)
                    dve.tensor_tensor(ropet[:, :, :], banks(rnd, s)[:, :, :].rearrange("p a (t s) -> p (a t) s", t=2),
                                      rope[:, 0:1, :].broadcast_to([P, 4, S]), ALU.mult).then_inc(read_out(rnd, s), 1)
                elif kind == "ROT":
                    unit_filled(dve, rnd, s)
                    for qk in range(2):
                        last = dve.tensor_tensor(split[:, 3 * qk, :, :],
                                                 banks(rnd, s)[:, qk, :].rearrange("p (t s) -> p t s", t=2),
                                                 rope[:, 1:2, :].broadcast_to([P, 2, S]), ALU.mult)
                    last.then_inc(read_out(rnd, s), 1)
                elif kind == "ROTLO":
                    wait(dve, qk_hi, layer, b, 1)
                    dve.tensor_tensor(split[:, 0:4:3, :, :].rearrange("p a b c -> p a (b c)").bitcast(F32R),
                                      ropet.rearrange("p (a t) s -> p a (t s)", t=2),
                                      split[:, 1:3, :, :].rearrange("p a b c -> p a (b c)"), ALU.subtract)\
                        .then_inc(qk_lo.handle, 1)
                    wait(dve, qk_lo, layer, b, 1)
                elif kind == "LNS":
                    ln_stats_of(layer, b, n)
                elif kind == "LNN":
                    normalise(layer, b, n)
                elif kind == "X":
                    wait(dve, x_hi, layer, b, 1)
                    dve.tensor_tensor(xT[:, 1, :, :].rearrange("p a b -> p (a b)"), banks(rnd, s)[:, 0, :],
                                      xT[:, 0, :, :].rearrange("p a b -> p (a b)").bitcast(F32), ALU.subtract)\
                        .then_inc(read_out(rnd, s), 1)
                elif kind == "RAW":
                    if last_of_layer0(layer, b):
                        late(0, N_LATE_B)
                elif kind == "LATE":
                    dve.wait_ge(raw_hi, b + 1)
                    dve.tensor_tensor(wD[:, 1, bass.ds(b * STREAM_CHUNK, STREAM_CHUNK)],
                                      big[:, n * SLOT:n * SLOT + STREAM_CHUNK],
                                      wD[:, 0, bass.ds(b * STREAM_CHUNK, STREAM_CHUNK)].bitcast(F32),
                                      ALU.subtract).then_inc(raw_lo, 1)
                    if last_of_layer0(layer, b):
                        late(N_LATE_B, len(LATE) - 1)
                elif kind == "LT":
                    unit_filled(dve, rnd, s)
                    dve.tensor_copy(lg[:, :, :], banks(rnd, s)[:, 0, 0:BLK * NE].rearrange("p (k e) -> p k e", k=BLK))\
                        .then_inc(read_out(rnd, s), 1)
                    unit_read(dve, rnd, s)
                    alone(dve, dve_passed)
                    for blk in range(BLK):
                        dve.max(m8[:, blk, :], lg[:, blk, :]).then_inc(top_step.handle, 1)
                    wait(dve, top_step, layer, b, 2)
                    alone(dve, dve_passed)
                    for blk in range(BLK):
                        dve.max_index(i8[:, blk, :], m8[:, blk, :], lg[:, blk, :]).then_inc(top_step.handle, 1)
                    dve.tensor_scalar(nmax[:, :], m8[:, :, 0], -1.0, None, ALU.mult).then_inc(top_step.handle, 1)
                    wait(dve, top_step, layer, b, 4)
                    dve.tensor_copy(i8f[:, :, :], i8[:, :, :]).then_inc(top_step.handle, 1)
                    wait(dve, top_step, layer, b, 6)
                    for blk in range(BLK):
                        dve.tensor_scalar(sel0[:, blk, :], iota[:, :], i8f[:, blk, 0:1], None, ALU.is_equal)\
                            .then_inc(top_step.handle, 1)
                    wait(dve, top_step, layer, b, 8)
                    for blk in range(BLK):
                        dve.scalar_tensor_tensor(sel1[:, blk, :], iota[:, :], i8f[:, blk, 1:2], sel0[:, blk, :],
                                                 ALU.is_equal, ALU.add).then_inc(top_step.handle, 1)
                    wait(dve, exps_done, layer, b, 2)
                    dve.reciprocal(rsum[:, :], esum[:, :]).then_inc(top_step.handle, 1)
                    wait(dve, top_step, layer, b, 11)
                    for blk in range(BLK):
                        for at in (0, 32):
                            dve.scalar_tensor_tensor(comb[:, blk, at:at + NE], ex[:, blk, :], rsum[:, blk:blk + 1],
                                                     sel1[:, blk, :], ALU.mult, ALU.mult).then_inc(comb_done.handle, 1)
                elif kind == "CT":
                    wait(dve, comb_hi, layer, b, 1)
                    dve.tensor_tensor(combT[32:40, :], banks(rnd, s)[32:40, 0, 0:S], combT[32:40, :].bitcast(F32),
                                      ALU.subtract).then_inc(read_out(rnd, s), 1)
                elif kind == "MAX":
                    unit_filled(dve, rnd, s)
                    heads = slice(j, H, NPAIR)
                    dve.tensor_reduce(mx[:, 0, heads], banks(rnd, s)[:, :, 0:P], AX.X, ALU.max)
                    dve.tensor_reduce(mx[:, 1, heads], banks(rnd, s)[:, :, S:2 * S], AX.X, ALU.max)\
                        .then_inc(read_out(rnd, s), 1)
                elif kind == "PV":
                    wait(dve, pv_done, layer, b, j + 1)
                    dve.tensor_copy(pvT[:, j, :], pv[:, 0, :]).then_inc(pv_out.handle, 1)
                elif kind == "TR":
                    unit_filled(dve, rnd, s)
                    heads = banks(rnd, s)[:, :, :].rearrange("p k (h d) -> p k h d", d=2 * HD)
                    dve.reciprocal(rden[:, :, :], heads[:, :, :, HD]).then_inc(den_done.handle, 1)
                    wait(dve, den_done, layer, b, 1)
                    dve.tensor_tensor(o_tok.rearrange("p k (h d) -> p k h d", h=H), heads[:, :, :, 0:HD],
                                      rden[:, :, :].unsqueeze(3).broadcast_to([P, BLK, H, HD]), ALU.mult)\
                        .then_inc(read_out(rnd, s), 1)
                elif kind == "OT":
                    wait(dve, o_hi, layer, b, 1)
                    dve.tensor_tensor(oT[:, 1, :, :].rearrange("p a b -> p (a b)"), banks(rnd, s)[:, 0, :],
                                      oT[:, 0, :, :].rearrange("p a b -> p (a b)").bitcast(F32), ALU.subtract)\
                        .then_inc(read_out(rnd, s), 1)
                elif kind == "PROJ":
                    wait(dve, acc_ready, layer, b, 1)
                    wait(dve, y_stored, layer, b, 0)
                    dve.tensor_tensor(yt[:, :, :], acc[:, :, :], xt[:, n, :, :], ALU.add).then_inc(y_done.handle, 1)
                    if last_of_layer0(layer, b):
                        late(len(LATE) - 1, len(LATE))
                elif kind == "G":
                    wait(dve, tanh_done, layer, b, j + 1)
                    dve.scalar_tensor_tensor(ga[:, j % 2, :], th[:, j % 2, :], 1.0, gu[j % 2][:, 0, :], ALU.add, ALU.mult)\
                        .then_inc(gate_done.handle, 1)
                    wait(dve, gate_done, layer, b, j + 1)
                    dve.scalar_tensor_tensor(hb[:, j % 2, :], ga[:, j % 2, :], 0.5, gu[j % 2][:, 1, :], ALU.mult,
                                             ALU.mult).then_inc(hid_done.handle, 1)
                elif kind == "H":
                    wait(dve, h_hi, layer, b, j + 1)
                    dve.tensor_tensor(hs[:, j % 3, 1, :], hb[:, j % 2, :], hs[:, j % 3, 0, :].bitcast(F32),
                                      ALU.subtract).then_inc(h_lo.handle, 1)

            walk(dve, step)

        @block.gpsimd
        def _(pool):
            prime(pool, "POOL")
            pool.memset(negh[:, :], -0.5).then_inc(neg_half_set, 1)
            pool.memset(comb[:, :, :], 0.0).then_inc(const_set, 1)
            pool.memset(vaug[:, :, :, :], 1.0).then_inc(const_set, 1)
            pool.memset(stkf[:, 1, :, :], 1.0).then_inc(const_set, 1)
            pool.wait_ge(neg_half_set, 1)

            def rstd_of(nl, nb):
                wait(pool, ln_stats, nl, nb, 4)
                alone(pool, pool_passed)
                pool.tensor_scalar(vareps[:, :], mv[:, :, 1], EPS, None, ALU.add).then_inc(ln_rstd.handle, 1)
                wait(pool, ln_rstd, nl, nb, 1)
                pool.tensor_tensor(rstd[:, :], vareps[:, :], negh[:, :], ALU.pow).then_inc(ln_rstd.handle, 1)

            rstd_of(0, 0)
            pool.wait_ge(idx_loaded[index_load_of(POOL_CHUNK)], 16)
            for k in range(LUT):
                pool.tensor_scalar(pool_sum[:, :] if k == 0 else pool_term[:, :],
                                   idx[:, POOL_CHUNK * CHUNK:(POOL_CHUNK + 1) * CHUNK], float(k), lut[:, k:k + 1],
                                   ALU.is_equal, ALU.mult).then_inc(pool_step, 1)
                if k:
                    pool.wait_ge(pool_step, 2 * k)
                    pool.tensor_tensor(pool_sum[:, :], pool_sum[:, :], pool_term[:, :], ALU.add).then_inc(pool_step, 1)
                    pool.wait_ge(pool_step, 2 * k + 1)

            def step(rnd, s, kind, j, batch):
                layer, b, n = batch
                if kind == "ROT":
                    unit_read(pool, rnd, s)
                    for qk in range(2):
                        last = pool.tensor_tensor(ropet[:, 2 * qk:2 * qk + 2, :], ropet[:, 2 * qk:2 * qk + 2, :],
                                                  split[:, 3 * qk, :, :], ALU.add)
                    last.then_inc(rope_sum.handle, 1)
                elif kind == "LNS":
                    rstd_of(layer, b)
                elif kind == "ST":
                    unit_read(pool, rnd, s)
                    alone(pool, pool_passed)
                    diag = prob_of(rnd[0], j)[:, 0:2].rearrange("p a r c -> p (a r) c")
                    pool.affine_select(out=diag, in_=diag, compare_op=ALU.is_ge, fill=0.0, base=0,
                                       pattern=[[0, 4], [1, P]], channel_multiplier=-1)\
                        .then_inc(masked.handle, 1)
                elif kind == "G" and layer == 1 and j >= TS:
                    wait(pool, hid_done, layer, b, j + 1)
                    if (j - TS) % 4 == 0:
                        unit_read(pool, rnd, f"CB{(j - TS) // 4}")
                    pool.tensor_tensor(hb[:, j % 2, :], hb[:, j % 2, :], combB[:, j - TS, :], ALU.mult)\
                        .then_inc(weighted.handle, 1)

            walk(pool, step)


def layout(a):
    f = np.float32
    order = np.array([(4 * jj + 2 * t + r) * HD + d for t in range(2) for jj in range(4) for r in range(2)
                      for d in range(HD)])
    rot = np.array([(o // HD) * HD + (o % HD + HD // 2) % HD for o in order])

    def rows(w):
        return np.ascontiguousarray(w.reshape(-1, P, w.shape[1]).transpose(1, 0, 2)).reshape(P, -1)

    def padded(w, n, fill=0):
        out = np.full((n,) + w.shape[1:], fill, w.dtype)
        out[:w.shape[0]] = w
        return out

    def gate_up(g, u):
        w = np.stack([g.reshape(-1, P, KT, P), u.reshape(-1, P, KT, P)])
        return np.ascontiguousarray(w.transpose(4, 1, 3, 0, 2)).reshape(P, -1)

    wqkv = a["L0_attn_W_qkv"]
    qkv0 = np.concatenate([wqkv[0:D][order], wqkv[D:2 * D][order], wqkv[2 * D:]]).T
    w0_lin = np.concatenate([rows(qkv0), rows(a["L0_attn_W_proj"].T)], axis=1)
    gi, ui, di = a["L0_ffn_gate_idx"], a["L0_ffn_up_idx"], a["L0_ffn_down_idx"]
    idx0 = np.concatenate([gate_up(padded(gi, T0 * P, LUT), padded(ui, T0 * P, LUT)),
                           rows(padded(np.ascontiguousarray(di.T), T0 * P, LUT))], axis=1)
    wq, wk, wv = a["L1_attn_Wq"], a["L1_attn_Wk"], a["L1_attn_Wv"]
    g1 = np.concatenate([padded(a["L1_ffn_sw1"], TS * P), a["L1_ffn_w1"].reshape(NE * EI, D)])
    u1 = np.concatenate([padded(a["L1_ffn_sw2"], TS * P), a["L1_ffn_w2"].reshape(NE * EI, D)])
    w1_stream = np.concatenate([rows(np.concatenate([wq[order], wk[order], wv]).T),
                                rows(padded(a["L1_ffn_gate_w"], P).T), gate_up(g1, u1)], axis=1)
    dn1 = np.concatenate([padded(np.ascontiguousarray(a["L1_ffn_sw3"].T), TS * P),
                          a["L1_ffn_w3"].transpose(0, 2, 1).reshape(NE * EI, D)])
    w1_late = np.concatenate([rows(dn1), rows(np.concatenate([wq[rot], wk[rot]]).T), rows(a["L1_attn_Wo"].T)], axis=1)

    inv_freq = 1.0 / 10000.0 ** (np.arange(0, HD, 2, dtype=f) / HD)
    freqs = np.einsum("i,j->ij", np.arange(S, dtype=f), inv_freq)
    emb = np.concatenate((freqs, freqs), axis=-1)
    d = np.arange(P) % HD
    sign = np.where(d < HD // 2, -1.0, 1.0).astype(f)[:, None]
    rope = np.stack([np.cos(emb).astype(f).T[d], np.sin(emb).astype(f).T[d] * sign], axis=1)
    q, k = np.arange(P)[:, None], np.arange(P)[None, :]
    mask = np.where(k > q, -1e30, 0.0).astype(f)
    owner = (np.arange(TE * P) // EI)[None, :]
    e = np.arange(64)[:, None]
    esel = (((e < NE) & (e == owner)) | ((e >= 32) & (e - 32 == owner))).astype(f)
    return {
        "x_in": a["L0_attn_x"], "w0_lin": w0_lin, "idx0": idx0, "lut_in": a["L0_ffn_lut"], "w1_stream": w1_stream,
        "w1_late": w1_late, "rope_in": rope.astype(f), "ident_in": np.eye(P, dtype=f),
        "mask_in": np.stack([mask, mask], axis=1).reshape(P, 2 * P), "esel_in": esel,
        "iota_in": np.tile(np.arange(NE, dtype=f), (P, 1)),
    }


def kernel(**inputs):
    import concourse.bacc as bacc
    from concourse.bass_utils import run_bass_kernel_spmd

    arrays = {n: np.ascontiguousarray(v) for n, v in layout({k: np.asarray(v) for k, v in inputs.items()}).items()}
    nc = bacc.Bacc("TRN2", target_bir_lowering=False, num_devices=1)
    args = {n: nc.dram_tensor(n, v.shape, mybir.dt.from_np(v.dtype), kind="ExternalInput").ap()
            for n, v in arrays.items()}
    y = nc.dram_tensor("y_out", (B, S, D), F32, kind="ExternalOutput").ap()
    build(nc, y_out=y, **args)
    r = run_bass_kernel_spmd(nc, [arrays], core_ids=[0])
    return r.results[0]["y_out"]
```
